# Optimizing a Trainium2 kernel written in Bass

```python
import numpy as np
import jax
import jax.numpy as jnp

def _softmax(x, axis=-1):
    return jax.nn.softmax(x, axis=axis)

def _gelu(x):
    return jax.nn.gelu(x, approximate=True)

def _silu(x):
    return jax.nn.silu(x)

def _sigmoid(x):
    return jax.nn.sigmoid(x)

def _layernorm(x, axis=-1, eps=1e-05):
    m = jnp.mean(x, axis=axis, keepdims=True)
    v = jnp.var(x, axis=axis, keepdims=True)
    return (x - m) / jnp.sqrt(v + eps)

def _scatter_add(tgt, idx, src, axis=0):
    return tgt.at[idx].add(src)

def _segment_sum(src, seg, n):
    return jax.ops.segment_sum(src, seg, n)
kernel_name = 'mk_recurrent_d1_jaxref_r8_0072ec'

def setup_inputs(seed: int=0):
    np.random.seed(seed)
    _w = jnp.asarray

    def _L0_attn_setup():
        import jax, jax.numpy as jnp
        import numpy as np
        B, T, D, H = (2, 256, 256, 16)
        DH = D // H
        ROPE_BASE = 10000.0

        def _rope(x, cos, sin):
            x0 = x[..., 0::2]
            x1 = x[..., 1::2]
            r0 = cos * x0 - sin * x1
            r1 = sin * x0 + cos * x1
            return jnp.stack((r0, r1), axis=-1).reshape(x.shape)
        key = jax.random.key(seed)
        ks = jax.random.split(key, 5)
        s = D ** (-0.5)
        return {'X': jax.random.normal(ks[0], (B, T, D), dtype=jnp.float32), 'Wq': jax.random.normal(ks[1], (D, D), dtype=jnp.float32) * s, 'Wk': jax.random.normal(ks[2], (D, D), dtype=jnp.float32) * s, 'Wv': jax.random.normal(ks[3], (D, D), dtype=jnp.float32) * s, 'Wo': jax.random.normal(ks[4], (D, D), dtype=jnp.float32) * s}
    _L0_attn_in = _L0_attn_setup()

    def _L0_ffn_setup():
        import jax, jax.numpy as jnp
        import numpy as np
        HIDDEN = 256
        INTER = 1024
        SCALE = 64.0

        def fwht(x):
            orig_shape = x.shape
            n = orig_shape[-1]
            x = x.reshape(-1, n)
            h = 1
            while h < n:
                x = x.reshape(-1, n // (2 * h), 2, h)
                a, b = (x[:, :, 0, :], x[:, :, 1, :])
                x = jnp.stack([a + b, a - b], axis=2).reshape(-1, n)
                h *= 2
            return (x / jnp.sqrt(jnp.asarray(n, x.dtype))).reshape(orig_shape)
        key = jax.random.key(seed)
        ks = jax.random.split(key, 8)
        inp = jax.random.normal(ks[0], (4, 256, HIDDEN), dtype=jnp.float32)
        SU_ug = jnp.where(jax.random.bernoulli(ks[1], 0.5, (HIDDEN,)), 1.0, -1.0).astype(jnp.float32)
        SU_dp = jnp.where(jax.random.bernoulli(ks[2], 0.5, (INTER,)), 1.0, -1.0).astype(jnp.float32)
        Wscale_ug = jax.random.uniform(ks[3], (2 * INTER,), jnp.float32, 0.5, 1.5)
        Wscale_dp = jax.random.uniform(ks[4], (HIDDEN,), jnp.float32, 0.5, 1.5)
        W_up = jax.random.normal(ks[5], (INTER, HIDDEN), dtype=jnp.float32) * 0.02
        W_gate = jax.random.normal(ks[6], (INTER, HIDDEN), dtype=jnp.float32) * 0.02
        W_down = jax.random.normal(ks[7], (HIDDEN, INTER), dtype=jnp.float32) * 0.02
        return {'input': inp, 'SU_ug': SU_ug, 'SU_dp': SU_dp, 'Wscale_ug': Wscale_ug, 'Wscale_dp': Wscale_dp, 'W_up': W_up, 'W_gate': W_gate, 'W_down': W_down}
    _L0_ffn_in = _L0_ffn_setup()
    _d = {'L0_attn_X': _L0_attn_in['X'], 'L0_attn_Wq': _L0_attn_in['Wq'], 'L0_attn_Wk': _L0_attn_in['Wk'], 'L0_attn_Wv': _L0_attn_in['Wv'], 'L0_attn_Wo': _L0_attn_in['Wo'], 'L0_ffn_SU_ug': _L0_ffn_in['SU_ug'], 'L0_ffn_SU_dp': _L0_ffn_in['SU_dp'], 'L0_ffn_Wscale_ug': _L0_ffn_in['Wscale_ug'], 'L0_ffn_Wscale_dp': _L0_ffn_in['Wscale_dp'], 'L0_ffn_W_up': _L0_ffn_in['W_up'], 'L0_ffn_W_gate': _L0_ffn_in['W_gate'], 'L0_ffn_W_down': _L0_ffn_in['W_down']}
    _x0 = _d['L0_attn_X']
    _d['L0_attn_X'] = jax.random.normal(jax.random.fold_in(jax.random.key(seed), 1), (4, 1024, 256), dtype=_x0.dtype)
    del _x0
    return _d

def reference(L0_attn_X, L0_attn_Wq, L0_attn_Wk, L0_attn_Wv, L0_attn_Wo, L0_ffn_SU_ug, L0_ffn_SU_dp, L0_ffn_Wscale_ug, L0_ffn_Wscale_dp, L0_ffn_W_up, L0_ffn_W_gate, L0_ffn_W_down):

    def _L0_attn_ref(X, Wq, Wk, Wv, Wo):
        import jax, jax.numpy as jnp
        import numpy as np
        B, T, D, H = (2, 256, 256, 16)
        DH = D // H
        ROPE_BASE = 10000.0

        def _rope(x, cos, sin):
            x0 = x[..., 0::2]
            x1 = x[..., 1::2]
            r0 = cos * x0 - sin * x1
            r1 = sin * x0 + cos * x1
            return jnp.stack((r0, r1), axis=-1).reshape(x.shape)
        b, t, d = X.shape
        Q = X @ Wq.T
        K = X @ Wk.T
        V = X @ Wv.T
        Qh = Q.reshape(b, t, H, DH).transpose(0, 2, 1, 3)
        Kh = K.reshape(b, t, H, DH).transpose(0, 2, 1, 3)
        Vh = V.reshape(b, t, H, DH).transpose(0, 2, 1, 3)
        theta = ROPE_BASE ** (-2.0 * jnp.arange(DH // 2, dtype=jnp.float32) / DH)
        angles = jnp.arange(t, dtype=jnp.float32)[:, None] * theta[None, :]
        cos = jnp.cos(angles).astype(X.dtype)
        sin = jnp.sin(angles).astype(X.dtype)
        Qr = _rope(Qh, cos, sin)
        Kr = _rope(Kh, cos, sin)
        scores = jnp.einsum('bhqd,bhkd->bhqk', Qr, Kr) * DH ** (-0.5)
        causal = jnp.triu(jnp.ones((t, t), dtype=bool), 1)
        scores = jnp.where(causal, jnp.finfo(scores.dtype).min, scores)
        pattern = jax.nn.softmax(scores, axis=-1)
        heads = jnp.einsum('bhqk,bhkd->bqhd', pattern, Vh).reshape(b, t, d)
        return heads @ Wo.T

    def _L0_ffn_ref(input, SU_ug, SU_dp, Wscale_ug, Wscale_dp, W_up, W_gate, W_down):
        import jax, jax.numpy as jnp
        import numpy as np
        HIDDEN = 256
        INTER = 1024
        SCALE = 64.0

        def fwht(x):
            orig_shape = x.shape
            n = orig_shape[-1]
            x = x.reshape(-1, n)
            h = 1
            while h < n:
                x = x.reshape(-1, n // (2 * h), 2, h)
                a, b = (x[:, :, 0, :], x[:, :, 1, :])
                x = jnp.stack([a + b, a - b], axis=2).reshape(-1, n)
                h *= 2
            return (x / jnp.sqrt(jnp.asarray(n, x.dtype))).reshape(orig_shape)
        n = SU_ug.shape[0]
        x = input.reshape(-1, n)
        x = fwht(x * SU_ug) / SCALE
        x_up = x @ W_up.T * (Wscale_ug[:INTER] * SCALE)
        x_gate = x @ W_gate.T * (Wscale_ug[INTER:] * SCALE)
        x = jax.nn.silu(x_gate) * x_up
        x = fwht(x * SU_dp) / SCALE
        x = x @ W_down.T * (Wscale_dp * SCALE)
        return x.reshape(input.shape)
    x = L0_attn_X
    xn = _layernorm(x, axis=-1)
    s = _L0_attn_ref(xn, L0_attn_Wq, L0_attn_Wk, L0_attn_Wv, L0_attn_Wo)
    g = _silu(_L0_ffn_ref(xn, L0_ffn_SU_ug, L0_ffn_SU_dp, L0_ffn_Wscale_ug, L0_ffn_Wscale_dp, L0_ffn_W_up, L0_ffn_W_gate, L0_ffn_W_down))
    x = x + s * g
    return x

_drawn_inputs = setup_inputs


def setup_inputs(seed=0):
    import zlib

    import numpy as np

    out = dict(_drawn_inputs(seed))
    spreads = {}
    factors = {}
    for name, (base, spread) in spreads.items():
        noise = np.random.default_rng([zlib.crc32(name.encode()), seed]).standard_normal(out[name].shape)
        drawn = base * np.exp(spread * noise) if base else spread * noise
        out[name] = jnp.asarray(drawn.astype(out[name].dtype))
    for name, factor in factors.items():
        out[name] = (out[name] * factor).astype(out[name].dtype)
    return out
```

```python
import concourse.bass as bass
from concourse import mybir
from contextlib import ExitStack

F32 = mybir.dt.float32
F32R = mybir.dt.float32r
BF16 = mybir.dt.bfloat16
ALU = mybir.AluOpType
ACT = mybir.ActivationFunctionType
AX = mybir.AxisListType

P = 128
B, T, D, H, DH = 4, 1024, 256, 16, 16
INTER = 1024
SCALE = DH ** -0.5
EPS = 1e-5
CH = 512
NTOK = B * T
NCHUNK = NTOK // CH
TPC = CH // P
DC = D // P
IB = INTER // P
TB = T // P
HG = 4
NG = H // HG
NU = B * NG
NPAIR = HG // 2
SLOT = 64
NEG = -1.0e30


class Sem:

    def __init__(self, handle, ahead=0):
        self.handle, self.ahead = handle, ahead

    def wait(self, eng, count):
        eng.wait_ge(self.handle, count + self.ahead)

    def wait_apart(self, eng, count, passed):
        self.wait(eng, count)
        eng.sem_inc(passed.handle, 1)

    def by(self, ins, n=1):
        ins.then_inc(self.handle, n)
        return ins

    def give(self, eng):
        if self.ahead:
            eng.sem_inc(self.handle, self.ahead)


class Chain:

    def __init__(self, eng, handle):
        self.eng, self.handle, self.base, self.per, self.k, self.it = eng, handle, 0, 0, 0, 0

    def link(self, ins):
        ins.then_inc(self.handle, 1)
        self.k += 1
        self.eng.wait_ge(self.handle, self.it * self.per + (self.base + self.k))

    def link_apart(self, ins, passed):
        self.link(ins)
        self.eng.sem_inc(passed.handle, 1)

    def enter(self, it, per):
        self.it, self.per = it, per
        self.base += self.k
        self.k = 0

    def leave(self, iterations):
        assert self.k == self.per, (self.k, self.per)
        self.base += self.per * iterations
        self.it, self.per, self.k = 0, 0, 0


def ffn_block(nc, ps, io, scr):
    x_d = io["x"].rearrange("(c t p) d -> c p t d", t=TPC, p=P)
    ctx = ExitStack()
    with ctx:
        sb = lambda name, shape, dt=F32: ctx.enter_context(nc.sbuf_tensor(name, shape, dt))
        sem = lambda name, ahead=0: Sem(ctx.enter_context(nc.semaphore(name)), ahead)

        ident = sb("ident", [P, P])
        had = sb("had", [P, P])
        cos = sb("cos", [P, TB, DH])
        sin = sb("sin", [P, TB, DH])
        su_ug = sb("su_ug", [P, DC])
        su_dp = sb("su_dp", [P, IB])
        ws_ug = sb("ws_ug", [P, 2 * IB])
        ws_dp = sb("ws_dp", [P, DC])
        wqkv_hi = sb("wqkv_hi", [P, DC, 3 * D], F32R)
        wqkv_lo = sb("wqkv_lo", [P, DC, 3 * D], F32R)
        wug_hi = sb("wug_hi", [P, DC, 2 * INTER], F32R)
        wug_lo = sb("wug_lo", [P, DC, 2 * INTER], F32R)
        wd_hi = sb("wd_hi", [P, IB, D], F32R)
        wd_lo = sb("wd_lo", [P, IB, D], F32R)
        x_sb = sb("x_sb", [P, 2, TPC, D])
        xn = sb("xn", [P, TPC, D])
        stats = sb("stats", [P, TPC, 6])
        moments = sb("moments", [P, TPC, 2])
        var_eps = sb("var_eps", [P, TPC])
        minus_half = sb("minus_half", [P, TPC])
        rstd = sb("rstd", [P, TPC])
        xh = [sb(f"xh{i}", [P, DC, CH], F32R) for i in range(2)]
        xl = [sb(f"xl{i}", [P, DC, CH], F32R) for i in range(2)]
        y_sb = sb("y_sb", [P, 2, DC, CH])
        NHB = 4
        silu = sb("silu", [P, 2, CH])
        hid = sb("hid", [P, 2, CH])

        raw = ExitStack()
        rsb = lambda name, shape, dt=F32: raw.enter_context(nc.sbuf_tensor(name, shape, dt))
        with raw:
            prep_weights(nc, ps, io, rsb, ident, had, cos, sin, su_ug, su_dp, ws_ug, ws_dp,
                         wqkv_hi, wqkv_lo, wug_hi, wug_lo, wd_hi, wd_lo, minus_half)
        hid_hi = sb("hid_hi", [P, NHB, CH], F32R)
        hid_lo = sb("hid_lo", [P, NHB, CH], F32R)
        qkv = [sb(f"qkv{i}", [P, NG, TPC, 3 * HG * DH]) for i in range(2)]
        rot_a = sb("rot_a", [P, 2 * H, DH])
        rot_b = sb("rot_b", [P, 2 * H, DH])

        x_in = [sem(f"x_in{i}") for i in range(2)]
        var_ok = sem("var_ok")
        rstd_ok = sem("rstd_ok")
        xn_ok = sem("xn_ok")
        xt_ok = sem("xt_ok")
        xh_ok = sem("xh_ok")
        xl_ok = sem("xl_ok")
        qkv_ok = sem("qkv_ok")
        rot_read = sem("rot_read", 1)
        rot_ok = sem("rot_ok", 1)
        v_ok = sem("v_ok", 1)
        qkv_out = [sem(f"qkv_out{i}", 16) for i in range(2)]
        gu_ok = sem("gu_ok")
        silu_ok = sem("silu_ok")
        hid_ok = sem("hid_ok", 2)
        hh_ok = sem("hh_ok")
        hl_ok = sem("hl_ok")
        down_ok = sem("down_ok", NHB)
        y_ok = sem("y_ok", 1)
        y_out = [sem(f"y_out{i}", 16) for i in range(2)]
        passed = sem("passed")
        dve_chain = ctx.enter_context(nc.semaphore("dve_chain"))

        block = ctx.enter_context(nc.Block())

        def load_x(eng, c, par):
            eng.dma_start(x_sb[:, par], x_d[c]).then_inc(x_in[par].handle, 16)

        @block.sync
        def _(eng):
            for s in (*qkv_out, *y_out):
                s.give(eng)
            load_x(eng, 0, 0)
            load_x(eng, 1, 1)
            with eng.Fori(0, NCHUNK // 2) as it:
                for par in range(2):
                    c = it * 2 + par
                    xn_ok.wait_apart(eng, c + 1, passed)
                    load_x(eng, (c + 2) % NCHUNK, par)
                    rot_ok.wait_apart(eng, TPC * (c + 1), passed)
                    v_ok.wait_apart(eng, TPC * (c + 1), passed)
                    eng.dma_start(scr["qkv"][it, :, :, TPC * par:TPC * (par + 1), :].rearrange("g p t n -> p g t n"),
                                  qkv[par][:, :, :, :]).then_inc(qkv_out[par].handle, 16)
                    y_ok.wait_apart(eng, c + 1, passed)
                    eng.dma_start(scr["gate"][c].rearrange("o p n -> p o n"), y_sb[:, par]).then_inc(y_out[par].handle, 16)
            for par in range(2):
                qkv_out[par].wait(eng, 16 * NCHUNK // 2)
                y_out[par].wait(eng, 16 * NCHUNK // 2)
                x_in[par].wait(eng, 16 * (NCHUNK // 2 + 1))

        @block.gpsimd
        def _(eng):
            def rsqrt(n):
                var_ok.wait(eng, n)
                rstd_ok.by(eng.tensor_tensor(rstd[:, :], var_eps[:, :], minus_half[:, :], op=ALU.pow))
            rsqrt(1)
            with eng.Fori(0, NCHUNK) as c:
                rsqrt(c + 2)

        @block.tensor
        def _(pe):
            def transposes(n, par):
                xn_ok.wait(pe, n + 1)
                for d in range(DC):
                    for t in range(TPC):
                        last = pe.transpose(ps[:, 6 + d, t * P:(t + 1) * P], xn[:, t, d * P:(d + 1) * P], ident[:, :])
                xt_ok.by(last)

            def split_product(out, terms):
                for n, (lhs, rhs) in enumerate(terms):
                    last = pe.matmul(out, lhs, rhs, start=(n == 0), stop=(n == len(terms) - 1))
                return last

            def project(c, par, t):
                n = TPC * c + t
                rot_read.wait(pe, n)
                v_ok.wait(pe, n)
                tok = slice(t * P, (t + 1) * P)
                for bank, cols in ((6, slice(0, 2 * D)), (7, slice(2 * D, 3 * D))):
                    last = split_product(ps[:, bank, 0:cols.stop - cols.start],
                                         [(a[:, d, tok], w[:, d, cols]) for d in range(DC)
                                          for a, w in ((xh[par], wqkv_hi), (xh[par], wqkv_lo), (xl[par], wqkv_hi))])
                qkv_ok.by(last)

            def up_gate(c, par, ib):
                n = IB * c + ib
                hid_ok.wait(pe, n - 1)
                for k in range(2):
                    cols = slice(k * INTER + ib * P, k * INTER + (ib + 1) * P)
                    last = split_product(ps[:, 2 * (ib % 2) + k, :],
                                         [(w[:, d, cols], a[:, d, :]) for d in range(DC)
                                          for w, a in ((wug_hi, xh[par]), (wug_hi, xl[par]), (wug_lo, xh[par]))])
                gu_ok.by(last)

            def down(c, ib):
                n = IB * c + ib
                hh_ok.wait(pe, n + 1)
                hl_ok.wait(pe, n + 1)
                if ib == 0:
                    y_ok.wait(pe, c)
                r = ib % NHB
                for o in range(DC):
                    cols = slice(o * P, (o + 1) * P)
                    for k, (w, h) in enumerate(((wd_hi, hid_hi), (wd_hi, hid_lo), (wd_lo, hid_hi))):
                        last = pe.matmul(ps[:, 4 + o, :], w[:, ib, cols], h[:, r, :],
                                         start=(ib == 0 and k == 0), stop=(ib == IB - 1 and k == 2))
                down_ok.by(last)

            transposes(0, 0)
            with pe.Fori(0, NCHUNK // 2) as it:
                for par in range(2):
                    c = it * 2 + par
                    xh_ok.wait(pe, c + 1)
                    xl_ok.wait(pe, c + 1)
                    for ib in range(IB):
                        up_gate(c, par, ib)
                        if ib == 1:
                            project(c, par, 0)
                        if ib == 3:
                            project(c, par, 1)
                        if ib == 5:
                            rot_read.wait(pe, TPC * c + 2)
                            v_ok.wait(pe, TPC * c + 2)
                            transposes(c + 1, 1 - par)
                        if ib >= 2:
                            down(c, ib - 2)
                    xh_ok.wait(pe, c + 2)
                    xl_ok.wait(pe, c + 2)
                    project(c, par, 2)
                    down(c, IB - 2)
                    project(c, par, 3)
                    down(c, IB - 1)

        @block.scalar
        def _(act):
            v_ok.give(act)
            y_ok.give(act)

            def take_xh(n, par):
                xt_ok.wait(act, n + 1)
                xh_ok.by(act.copy(xh[par][:, :, :], ps[:, 6:8, :]))

            def take_v(c, par, t):
                qkv_ok.wait(act, TPC * c + t + 1)
                if t == 0:
                    qkv_out[par].wait(act, 8 * (c - par))
                v_ok.by(act.copy(qkv[par][:, :, t, 2 * HG * DH:],
                                 ps[:, 7, 0:D].rearrange("p (g n) -> p g n", g=NG)))

            take_xh(0, 0)
            with act.Fori(0, NCHUNK // 2) as it:
                for par in range(2):
                    c = it * 2 + par
                    for ib in range(IB):
                        n = IB * c + ib
                        gu_ok.wait(act, n + 1)
                        silu_ok.by(act.activation(silu[:, ib % 2, :], ps[:, 2 * (ib % 2) + 1, :], ACT.Silu,
                                                  scale=ws_ug[:, IB + ib:IB + ib + 1]))
                        hid_ok.wait(act, n + 1)
                        down_ok.wait(act, n - NHB + 1)
                        hh_ok.by(act.copy(hid_hi[:, ib % NHB, :], hid[:, ib % 2, :]))
                        if ib == 1:
                            take_v(c, par, 0)
                        if ib == 3:
                            take_v(c, par, 1)
                        if ib == 5:
                            take_xh(c + 1, 1 - par)
                    take_v(c, par, 2)
                    take_v(c, par, 3)
                    down_ok.wait(act, IB * (c + 1))
                    y_out[par].wait(act, 8 * (c - par))
                    for o in range(DC):
                        last = act.activation(y_sb[:, par, o, :], ps[:, 4 + o, :], ACT.Silu, scale=ws_dp[:, o:o + 1])
                    y_ok.by(last)

        @block.vector
        def _(dve):
            rot_read.give(dve)
            rot_ok.give(dve)
            hid_ok.give(dve)
            down_ok.give(dve)
            ch = Chain(dve, dve_chain)

            def layernorm(n, par, nth):
                x_in[par].wait(dve, 16 * (nth + 1))
                for t in range(TPC):
                    last = dve.bn_stats(stats[:, t, :], x_sb[:, par, t, :])
                ch.link_apart(last, passed)
                for t in range(TPC):
                    last = dve.bn_aggr(moments[:, t, :], stats[:, t, :])
                ch.link(last)
                var_ok.by(dve.tensor_scalar_add(var_eps[:, :], moments[:, :, 1], EPS))
                rstd_ok.wait(dve, n + 1)
                for t in range(TPC):
                    last = dve.tensor_scalar(xn[:, t, :], x_sb[:, par, t, :], moments[:, t, 0:1], rstd[:, t:t + 1],
                                             ALU.subtract, ALU.mult)
                xn_ok.by(last)

            def take_xl(n, par):
                xt_ok.wait(dve, n + 1)
                xh_ok.wait(dve, n + 1)
                xl_ok.by(dve.tensor_tensor(xl[par][:, :, :], ps[:, 6:8, :], xh[par][:, :, :].bitcast(F32), op=ALU.subtract))

            def rotate(c, par, t):
                tb = TPC * par + t
                qkv_ok.wait(dve, TPC * c + t + 1)
                src = ps[:, 6, :].rearrange("p (h d) -> p h d", d=DH)
                pairs = ps[:, 6, :].rearrange("p (h d two) -> p h d two", d=DH // 2, two=2)
                sins = sin[:, tb, :].rearrange("p (d two) -> p d two", two=2)
                b_out = rot_b[:, :, :].rearrange("p h (d two) -> p h d two", two=2)
                rot_ok.wait(dve, TPC * c + t)
                dve.tensor_tensor(rot_a[:, :, :], src, cos[:, tb:tb + 1, :].to_broadcast([P, 2 * H, DH]), op=ALU.mult)
                for k in range(2):
                    s = sins[:, :, k].rearrange("p (one d) -> p one d", one=1).to_broadcast([P, 2 * H, DH // 2])
                    last = dve.tensor_tensor(b_out[:, :, :, k], pairs[:, :, :, 1 - k], s, op=ALU.mult)
                rot_read.by(last)
                rot_read.wait(dve, TPC * c + t + 1)
                if t == 0:
                    qkv_out[par].wait(dve, 8 * (c - par))
                for k in range(2):
                    half = slice(k * H, (k + 1) * H)
                    dst = qkv[par][:, :, t, k * HG * DH:(k + 1) * HG * DH]
                    last = dve.tensor_tensor(dst,
                                             rot_a[:, half, :].rearrange("p (g h) d -> p g (h d)", g=NG),
                                             rot_b[:, half, :].rearrange("p (g h) d -> p g (h d)", g=NG), op=ALU.add)
                rot_ok.by(last)

            layernorm(0, 0, 0)
            take_xl(0, 0)
            with dve.Fori(0, NCHUNK // 2) as it:
                ch.enter(it, 4)
                for par in range(2):
                    c = it * 2 + par
                    for ib in range(IB):
                        n = IB * c + ib
                        gu_ok.wait(dve, n + 1)
                        silu_ok.wait(dve, n + 1)
                        hid_ok.by(dve.scalar_tensor_tensor(hid[:, ib % 2, :], ps[:, 2 * (ib % 2), :],
                                                           ws_ug[:, ib:ib + 1], silu[:, ib % 2, :], ALU.mult, ALU.mult))
                        hh_ok.wait(dve, n + 1)
                        hid_ok.wait(dve, n + 1)
                        hl_ok.by(dve.tensor_tensor(hid_lo[:, ib % NHB, :], hid[:, ib % 2, :],
                                                   hid_hi[:, ib % NHB, :].bitcast(F32), op=ALU.subtract))
                        if ib == 1:
                            rotate(c, par, 0)
                        if ib == 3:
                            rotate(c, par, 1)
                        if ib == 4:
                            layernorm(c + 1, 1 - par, it + par)
                        if ib == 5:
                            take_xl(c + 1, 1 - par)
                    rotate(c, par, 2)
                    rotate(c, par, 3)
            ch.leave(NCHUNK // 2)


def prep_weights(nc, ps, io, sb, ident, had, cos, sin, su_ug, su_dp, ws_ug, ws_dp,
                 wqkv_hi, wqkv_lo, wug_hi, wug_lo, wd_hi, wd_lo, minus_half):
    ctx = ExitStack()
    with ctx:
        sem = lambda name: Sem(ctx.enter_context(nc.semaphore(name)))
        wqkv = sb("wqkv_raw", [P, DC, 3 * D])
        wug = sb("wug_raw", [P, DC, 2 * INTER])
        wug_f = sb("wug_fold", [P, DC, 2 * INTER])
        wd = sb("wd_raw", [P, 2, IB, D])
        su_ug_s = sb("su_ug_s", [P, DC])
        su_dp_s = sb("su_dp_s", [P, IB])
        small_in, qkv_in, ug_in, d_in = sem("small_in"), sem("qkv_in"), sem("ug_in"), sem("d_in")
        ones_ok, ident_ok = sem("ones_ok"), sem("ident_ok")
        scale_ok = sem("scale_ok")
        ug_fold, d_fold = sem("ug_fold"), sem("d_fold")
        wq_hi = sem("wq_hi")
        prod, hi_ok, lo_ok = sem("prod"), sem("hi_ok"), sem("lo_ok")
        wq_lo = sem("wq_lo")
        NUG = DC * 2 * INTER // CH
        ND = IB * D // CH
        LOADS = 8
        block = ctx.enter_context(nc.Block())

        @block.sync
        def _(eng):
            eng.dma_start(wug[:, :, :], io["wug"].rearrange("(c p) n -> p c n", p=P)).then_inc(ug_in.handle, 16)
            eng.dma_start(wd[:, 0], io["wd"].rearrange("(c p) n -> p c n", p=P)).then_inc(d_in.handle, 16)

        @block.scalar
        def _(act):
            act.dma_start(wqkv[:, :, :], io["wqkv"].rearrange("(c p) n -> p c n", p=P)).then_inc(qkv_in.handle, 16)
            for dst, src in ((had, "had"), (cos, "cos"), (sin, "sin"), (su_ug, "su_ug"), (su_dp, "su_dp"),
                             (ws_ug, "ws_ug"), (ws_dp, "ws_dp")):
                full = tuple(slice(None) for _ in dst.shape)
                act.dma_start(dst[full], io[src]).then_inc(small_in.handle, 16)
            qkv_in.wait(act, 16)
            wq_hi.by(act.copy(wqkv_hi[:, :, :], wqkv[:, :, :]))
            scale_ok.wait(act, 2)
            for n in range(NUG + ND):
                prod.wait(act, n + 1)
                bank = ps[:, n % 8, :]
                if n < NUG:
                    o, cols = n // (NUG // DC), slice(n % (NUG // DC) * CH, (n % (NUG // DC) + 1) * CH)
                    last = act.mul(wug_hi[:, o, cols], bank, su_ug_s[:, o:o + 1])
                else:
                    for k in range(CH // D):
                        ib = (n - NUG) * (CH // D) + k
                        last = act.mul(wd_hi[:, ib, :], bank[:, k * D:(k + 1) * D], su_dp_s[:, ib:ib + 1])
                hi_ok.by(last)

        @block.gpsimd
        def _(eng):
            ones_ok.by(eng.memset(ident[:, :], 0.0))
            eng.memset(minus_half[:, :], -0.5)
            ones_ok.wait(eng, 1)
            ident_ok.by(eng.affine_select(out=ident[:, :], in_=ident[:, :], compare_op=ALU.not_equal, fill=1.0, base=0,
                                          pattern=[[-1, P]], channel_multiplier=1))

        @block.tensor
        def _(pe):
            small_in.wait(pe, 16 * 7)
            for n in range(NUG + ND):
                if n >= 8:
                    lo_ok.wait(pe, n - 7)
                if n < NUG:
                    o, k = n // (NUG // DC), n % (NUG // DC)
                    ug_fold.wait(pe, o + 1)
                    rhs = wug_f[:, o, k * CH:(k + 1) * CH]
                else:
                    d_fold.wait(pe, 3)
                    k = (n - NUG) * (CH // D)
                    rhs = wd[:, 1, k:k + CH // D, :]
                prod.by(pe.matmul(ps[:, n % 8, :], had[:, :], rhs, start=True, stop=True))

        @block.vector
        def _(dve):
            small_in.wait(dve, 16 * 7)
            scale_ok.by(dve.tensor_scalar_mul(su_ug_s[:, :], su_ug[:, :], float(D) ** -0.5))
            scale_ok.by(dve.tensor_scalar_mul(su_dp_s[:, :], su_dp[:, :], float(INTER) ** -0.5))
            ug_in.wait(dve, 16)
            for o, op in ((0, ALU.add), (1, ALU.subtract)):
                ug_fold.by(dve.tensor_tensor(wug_f[:, o, :], wug[:, 0, :], wug[:, 1, :], op=op))
            d_in.wait(dve, 16)
            for stage in range(3):
                step = 1 << stage
                if stage:
                    d_fold.wait(dve, stage)
                src, dst = (wd[:, i].rearrange("p (a two b) n -> p a two b n", two=2, b=step)
                            for i in (stage % 2, 1 - stage % 2))
                for o, op in ((0, ALU.add), (1, ALU.subtract)):
                    last = dve.tensor_tensor(dst[:, :, o], src[:, :, 0], src[:, :, 1], op=op)
                d_fold.by(last)
            wq_hi.wait(dve, 1)
            dve.tensor_tensor(wqkv_lo[:, :, :], wqkv[:, :, :], wqkv_hi[:, :, :].bitcast(F32), op=ALU.subtract)
            for n in range(NUG + ND):
                hi_ok.wait(dve, n + 1)
                bank = ps[:, n % 8, :]
                if n < NUG:
                    o, cols = n // (NUG // DC), slice(n % (NUG // DC) * CH, (n % (NUG // DC) + 1) * CH)
                    last = dve.scalar_tensor_tensor(wug_lo[:, o, cols], bank, su_ug_s[:, o:o + 1],
                                                    wug_hi[:, o, cols].bitcast(F32), ALU.mult, ALU.subtract)
                else:
                    for k in range(CH // D):
                        ib = (n - NUG) * (CH // D) + k
                        last = dve.scalar_tensor_tensor(wd_lo[:, ib, :], bank[:, k * D:(k + 1) * D],
                                                        su_dp_s[:, ib:ib + 1], wd_hi[:, ib, :].bitcast(F32),
                                                        ALU.mult, ALU.subtract)
                lo_ok.by(last)


def attention_block(nc, ps, io, scr):
    QC = T // CH
    STEPS = [(c, j) for c in range(QC) for j in range(TPC * (c + 1))]
    NS = len(STEPS)
    LAG = 2
    RING = 3
    first = lambda c, j: max(0, P * j - CH * c)
    diagonal = lambda c, j: P * j >= CH * c

    TILES = []
    for i in range(TB):
        for part in range(i // TPC + 1):
            w = min(P * (i + 1) - CH * part, CH)
            TILES += [(i, part, w, hs) for hs in (((0, 2), (1, 3)) if 2 * w <= CH else ((0,), (1,), (2,), (3,)))]
    NT = len(TILES)
    A_TILES = sum(i < TPC for i, _, _, _ in TILES)
    assert NT % 2 == 0
    PER_STEP = [0, 4, 4, 4, 4, 4, 4, 4, 4, 2, 2, 1]
    PIECE = [sum(PER_STEP[:s]) for s in range(NS + 1)]

    ctx = ExitStack()
    with ctx:
        sb = lambda name, shape, dt=F32: ctx.enter_context(nc.sbuf_tensor(name, shape, dt))
        sem = lambda name, ahead=0: Sem(ctx.enter_context(nc.semaphore(name)), ahead)

        ident = sb("a_ident", [P, P])
        ident_b = sb("a_ident_b", [P, P], BF16)
        mask = sb("a_mask", [P, P], BF16)
        loaded = sb("loaded", [P, TB, 3 * HG * DH])
        slots = sb("slots", [P, TB, 2 * HG, SLOT])
        qk_t = [sb(f"qk_t{i}", [P, 2 * NPAIR, T], F32R) for i in range(2)]
        v_ones = [sb(f"v_ones{i}", [P, TB, HG, 2 * DH]) for i in range(2)]
        probs = sb("probs", [P, RING, NPAIR, 2, CH])
        maxes = sb("maxes", [P, QC, TB, HG])
        maxes_b = sb("maxes_b", [P, TPC, HG])
        shift = [sb(f"shift{c}", [TPC * HG, P], F32R) for c in range(QC)]
        o_raw = [sb(f"o_raw{c}", [P, CH]) for c in range(QC)]
        o_inv = sb("o_inv", [P, QC, TPC, HG])
        o_nat = [sb(f"o_nat{c}", [P, TPC, HG * DH]) for c in range(QC)]

        passed = sem("a_passed")
        consts = sem("a_consts")
        loaded_ok = sem("loaded_ok")
        hi_ok, lo_ok = sem("slots_hi"), sem("slots_lo")
        v_ok = sem("v_ones_ok")
        t_ok, t_read = sem("t_ok"), sem("t_read")
        tile_ok, tile_read = sem("tile_ok"), sem("tile_read", 2)
        maxb_ok = sem("maxb_ok")
        mt_ok, mt_read = sem("mt_ok"), sem("mt_read")
        row_in = [sem(f"row_in{c}", 64) for c in range(QC)]
        st_ok, exp_ok = sem("st_ok"), sem("exp_ok", 2)
        sel_ok = sem("sel_ok")
        pv_ok = sem("pv_ok", RING)
        o_read = sem("o_read", 1)
        ot_ok, o_ok = sem("ot_ok"), sem("o_ok")
        inv_ok = sem("inv_ok")
        o_out = [sem(f"o_out{c}", 16) for c in range(QC)]
        S_BANK, PV_BANK, MAX_BANK, X_BANK = 0, 4, 5, 7
        NDIAG = sum(diagonal(*s) for s in STEPS)

        block = ctx.enter_context(nc.Block())

        def units(eng, slot):
            with eng.Fori(0, NU // 2 - 1) as it:
                for par in range(2):
                    slot(it * 2 + par, par, True, True, it)
            slot(NU - 2, 0, True, False, NU // 2 - 1)
            slot(NU - 1, 1, False, False, NU // 2 - 1)

        @block.sync
        def _(eng):
            for s in (*row_in, *o_out):
                s.give(eng)

            def load(v, b, g):
                if not isinstance(v, int) or v > 0:
                    hi_ok.wait(eng, v)
                    lo_ok.wait(eng, v)
                    v_ok.wait_apart(eng, v, passed)
                loaded_ok.by(eng.dma_start(loaded[:, :, :], scr["qkv"][b, g]), 16)

            def rows(v, par, c):
                mt_read.wait(eng, QC * v + c + 1)
                for h in range(HG):
                    row = SLOT * (h % 2) + 2 * DH
                    row_in[c].by(eng.dma_start(qk_t[par][row:row + 1, h // 2, c * CH:(c + 1) * CH].bitcast(F32),
                                               shift[c][h:h + HG * (TPC - 1) + 1:HG, :].bitcast(F32)), 16)

            def store(u, c, b, g):
                o_ok.wait_apart(eng, QC * u + c + 1, passed)
                dst = scr["heads"][b * QC + c, :, :, g, :]
                o_out[c].by(eng.dma_start(dst, o_nat[c][:, :, :]), 16)

            load(0, 0, 0)
            load(1, 0, 1)
            rows(0, 0, 0)
            rows(0, 0, 1)

            def slot(u, par, nxt, nxt2, it):
                b = it // 2 if isinstance(it, int) else it // 2
                g = (it % 2) * 2 + par
                if nxt2:
                    load(u + 2, (it + 1) // 2, ((it + 1) % 2) * 2 + par)
                if nxt:
                    rows(u + 1, 1 - par, 0)
                store(u, 0, b, g)
                store(u, 1, b, g)
                if nxt:
                    rows(u + 1, 1 - par, 1)
            units(eng, slot)
            for c in range(QC):
                o_out[c].wait(eng, 16 * NU)

        @block.gpsimd
        def _(eng):
            consts.by(eng.memset(ident[:, :], 0.0))
            consts.by(eng.memset(mask[:, :], 0.0))
            for i in range(2):
                eng.memset(v_ones[i][:, :, :, DH:], 1.0)
            consts.by(eng.memset(slots[:, :, :, 2 * DH:3 * DH], 0.0))
            consts.wait(eng, 3)
            consts.by(eng.affine_select(out=ident[:, :], in_=ident[:, :], compare_op=ALU.not_equal, fill=1.0, base=0,
                                        pattern=[[-1, P]], channel_multiplier=1))
            consts.by(eng.affine_select(out=mask[:, :], in_=mask[:, :], compare_op=ALU.is_ge, fill=NEG, base=0,
                                        pattern=[[-1, P]], channel_multiplier=1))
            consts.by(eng.memset(slots[:, :, HG:, 2 * DH:2 * DH + 1], 1.0))
            consts.wait(eng, 6)
            consts.by(eng.tensor_copy(ident_b[:, :], ident[:, :]))

            def slot(u, par, nxt, nxt2, it):
                for s, (c, j) in enumerate(STEPS):
                    if diagonal(c, j):
                        for p in range(NPAIR):
                            exp_ok.wait_apart(eng, NPAIR * (NS * u + s) + p + 1, passed)
                            r = (NS * par + s) % RING
                            v = probs[:, r, p, :, 0:P]
                            sel_ok.by(eng.affine_select(out=v, in_=v, compare_op=ALU.is_ge, fill=0.0, base=0,
                                                        pattern=[[0, 2], [1, P]], channel_multiplier=-1))
            units(eng, slot)

        @block.tensor
        def _(pe):
            free = []

            def scratch():
                for s, n in free:
                    s.wait(pe, n)
                free.clear()

            def to_rows(v, tb):
                scratch()
                if tb == 0:
                    hi_ok.wait(pe, v + 1)
                    lo_ok.wait(pe, v + 1)
                for x in range(2 * NPAIR):
                    last = pe.transpose(ps[:, X_BANK, x * P:(x + 1) * P],
                                        slots[:, tb, 2 * x:2 * x + 2, :].rearrange("p a b -> p (a b)"), ident[:, :])
                t_ok.by(last)
                free.append((t_read, TB * v + tb + 1))

            def max_tile(v, par, k):
                i, part, w, heads = TILES[k]
                t_read.wait(pe, TB * v + i + 1)
                tile_read.wait(pe, NT * v + k - 1)
                bank = MAX_BANK + k % 2
                for n, h in enumerate(heads):
                    rows = slice(SLOT * (h % 2), SLOT * (h % 2 + 1))
                    masked = part == i // TPC
                    last = pe.matmul(ps[:, bank, n * w:(n + 1) * w], qk_t[par][rows, h // 2, i * P:(i + 1) * P],
                                     qk_t[par][rows, NPAIR + h // 2, part * CH:part * CH + w],
                                     start=True, stop=not masked)
                    if masked:
                        last = pe.matmul(ps[:, bank, (n + 1) * w - P:(n + 1) * w], ident_b[:, :], mask[:, :],
                                         start=False, stop=True)
                tile_ok.by(last)

            def max_rows(v, c):
                scratch()
                if c == 0:
                    tile_read.wait(pe, NT * v + A_TILES)
                    m = maxes[:, 0, 0:TPC, :]
                else:
                    maxb_ok.wait(pe, v + 1)
                    m = maxes_b[:, :, :]
                mt_ok.by(pe.transpose(ps[0:TPC * HG, X_BANK, 0:P], m.rearrange("p a b -> p (a b)"), ident[:, :]))
                free.append((mt_read, QC * v + c + 1))

            def scores(u, par, s, p):
                c, j = STEPS[s]
                exp_ok.wait(pe, NPAIR * (NS * u + s - 1) + p + 1)
                if j == 0 and p == 0:
                    row_in[c].wait(pe, 16 * HG * (u + 1))
                q0 = CH * c + first(c, j)
                for e in range(2):
                    rows = slice(SLOT * e, SLOT * (e + 1))
                    last = pe.matmul(ps[:, S_BANK + 2 * p + e, 0:CH - first(c, j)],
                                     qk_t[par][rows, NPAIR + p, j * P:(j + 1) * P],
                                     qk_t[par][rows, p, q0:(c + 1) * CH], start=True, stop=True)
                st_ok.by(last)

            def weigh(u, par, s):
                c, j = STEPS[s]
                exp_ok.wait(pe, NPAIR * (NS * u + s + 1))
                if diagonal(c, j):
                    d = sum(diagonal(*x) for x in STEPS[:s + 1])
                    sel_ok.wait(pe, NPAIR * (NDIAG * u + d))
                if s == 0:
                    v_ok.wait(pe, u + 1)
                if j == 0:
                    o_read.wait(pe, QC * u + c)
                r = (NS * par + s) % RING
                for h in range(HG):
                    last = pe.matmul(ps[2 * DH * h:2 * DH * (h + 1), PV_BANK, first(c, j):CH], v_ones[par][:, j, h, :],
                                     probs[:, r, h // 2, h % 2, 0:CH - first(c, j)],
                                     start=(j == 0), stop=(j == TPC * (c + 1) - 1))
                pv_ok.by(last)

            def to_tokens(u, c):
                scratch()
                o_read.wait(pe, QC * u + c + 1)
                for t in range(TPC):
                    last = pe.transpose(ps[:, X_BANK, t * P:(t + 1) * P], o_raw[c][:, t * P:(t + 1) * P], ident[:, :])
                ot_ok.by(last)
                free.append((o_ok, QC * u + c + 1))

            consts.wait(pe, 7)
            for tb in range(TB):
                to_rows(0, tb)
                for k in range(NT):
                    if TILES[k][0] == tb - 1:
                        max_tile(0, 0, k)
                if tb == TPC + 1:
                    max_rows(0, 0)
            for k in range(NT):
                if TILES[k][0] == TB - 1:
                    max_tile(0, 0, k)
            max_rows(0, 1)

            def slot(u, par, nxt, nxt2, it):
                v, vpar = u + 1, 1 - par
                free[:] = [(mt_read, QC * (u + 1))]
                for s in range(NS):
                    k = PIECE[s]
                    tiles = list(range(k, PIECE[s + 1])) if nxt else []
                    if nxt and s < TB // 2:
                        to_rows(v, 2 * s)
                    scores(u, par, s, 0)
                    for k in tiles[:2]:
                        max_tile(v, vpar, k)
                    scores(u, par, s, 1)
                    if nxt and s < TB // 2:
                        to_rows(v, 2 * s + 1)
                    for k in tiles[2:3]:
                        max_tile(v, vpar, k)
                    if s >= LAG:
                        weigh(u, par, s - LAG)
                    for k in tiles[3:]:
                        max_tile(v, vpar, k)
                    if nxt and s == 5:
                        max_rows(v, 0)
                    if s == 7:
                        to_tokens(u, 0)
                for s in range(NS - LAG, NS):
                    weigh(u, par, s)
                if nxt:
                    for k in range(PIECE[NS], NT):
                        max_tile(v, vpar, k)
                to_tokens(u, 1)
                if nxt:
                    max_rows(v, 1)
            units(pe, slot)

        @block.scalar
        def _(act):
            exp_ok.give(act)
            o_read.give(act)

            def make_hi(v):
                loaded_ok.wait(act, 16 * (v + 1))
                if not isinstance(v, int) or v > 0:
                    t_ok.wait(act, TB * v)
                qk = loaded[:, :, 0:2 * HG * DH].rearrange("p t (h d) -> p t h d", d=DH)
                act.copy(slots[:, :, :, 0:DH].bitcast(F32R), qk)
                act.copy(slots[:, :, 0:HG, DH:2 * DH].bitcast(F32R), qk[:, :, 0:HG, :])
                hi_ok.by(act.copy(slots[:, :, HG:, 3 * DH:].bitcast(F32R), qk[:, :, HG:, :]))

            def take_v(v, par):
                src = loaded[:, :, 2 * HG * DH:].rearrange("p t (h d) -> p t h d", d=DH)
                v_ok.by(act.copy(v_ones[par][:, :, :, 0:DH], src))

            def take_rows(v, par, tb):
                t_ok.wait(act, TB * v + tb + 1)
                t_read.by(act.copy(qk_t[par][:, :, tb * P:(tb + 1) * P],
                                   ps[:, X_BANK, :].rearrange("p (x n) -> p x n", x=2 * NPAIR)))

            def take_max(v, c):
                mt_ok.wait(act, QC * v + c + 1)
                row_in[c].wait(act, 16 * HG * v)
                mt_read.by(act.mul(shift[c][:, :], ps[0:TPC * HG, X_BANK, 0:P], -1.0))

            def exponentials(u, par, s, p):
                c, j = STEPS[s]
                w = CH - first(c, j)
                st_ok.wait(act, NPAIR * (NS * u + s) + p + 1)
                pv_ok.wait(act, NS * u + s - RING + 1)
                bank = S_BANK + 2 * p
                exp_ok.by(act.activation(probs[:, (NS * par + s) % RING, p, :, 0:w], ps[:, bank:bank + 2, 0:w],
                                         ACT.Exp, scale=SCALE))

            def take_o(u, c):
                pv_ok.wait(act, NS * u + (TPC if c == 0 else NS))
                o_read.by(act.copy(o_raw[c][:, :], ps[:, PV_BANK, :]))

            consts.wait(act, 7)
            make_hi(0)
            take_v(0, 0)
            for tb in range(TB):
                take_rows(0, 0, tb)
                if tb == TPC + 1:
                    take_max(0, 0)
            make_hi(1)
            take_max(0, 1)

            def slot(u, par, nxt, nxt2, it):
                v, vpar = u + 1, 1 - par
                if nxt:
                    take_v(v, vpar)
                for s in range(NS):
                    if nxt and s < TB // 2:
                        take_rows(v, vpar, 2 * s)
                    exponentials(u, par, s, 0)
                    exponentials(u, par, s, 1)
                    if nxt and s < TB // 2:
                        take_rows(v, vpar, 2 * s + 1)
                    if nxt and s == 5:
                        take_max(v, 0)
                    if s == 5:
                        take_o(u, 0)
                    if nxt2 and s == 8:
                        make_hi(v + 1)
                take_o(u, 1)
                if nxt:
                    take_max(v, 1)
            units(act, slot)

        @block.vector
        def _(dve):
            tile_read.give(dve)
            pv_ok.give(dve)

            def make_lo(v):
                hi_ok.wait(dve, v + 1)
                qk = loaded[:, :, 0:2 * HG * DH].rearrange("p t (h d) -> p t h d", d=DH)
                dve.tensor_tensor(slots[:, :, 0:HG, 3 * DH:].bitcast(F32R), qk[:, :, 0:HG, :], slots[:, :, 0:HG, 0:DH],
                                  op=ALU.subtract)
                lo_ok.by(dve.tensor_tensor(slots[:, :, HG:, DH:2 * DH].bitcast(F32R), qk[:, :, HG:, :],
                                           slots[:, :, HG:, 0:DH], op=ALU.subtract))

            def read_tile(v, k):
                i, part, w, heads = TILES[k]
                tile_ok.wait(dve, NT * v + k + 1)
                n = len(heads)
                tile_read.by(dve.tensor_reduce(maxes[:, part, i, heads[0]:heads[-1] + 1:2],
                                               ps[:, MAX_BANK + k % 2, 0:n * w].rearrange("p (h k) -> p h k", h=n),
                                               axis=AX.X, op=ALU.max))

            def both_parts(v):
                tile_read.wait(dve, NT * (v + 1))
                maxb_ok.by(dve.tensor_tensor(maxes_b[:, :, :], maxes[:, 0, TPC:, :], maxes[:, 1, TPC:, :], op=ALU.max))

            def normalise(u, c):
                ot_ok.wait(dve, QC * u + c + 1)
                rows = ps[:, X_BANK, :].rearrange("p (t h d) -> p t h d", t=TPC, d=2 * DH)
                inv = o_inv[:, c]
                inv_ok.by(dve.reciprocal(inv, rows[:, :, :, DH]))
                inv_ok.wait(dve, QC * u + c + 1)
                o_out[c].wait(dve, 16 * u)
                o_ok.by(dve.tensor_tensor(o_nat[c][:, :, :].rearrange("p t (h d) -> p t h d", d=DH), rows[:, :, :, 0:DH],
                                          inv.rearrange("p t (h one) -> p t h one", one=1)
                                          .to_broadcast([P, TPC, HG, DH]), op=ALU.mult))

            make_lo(0)
            for k in range(NT):
                read_tile(0, k)
            both_parts(0)
            make_lo(1)

            def slot(u, par, nxt, nxt2, it):
                v = u + 1
                for s in range(NS):
                    if nxt:
                        for k in range(PIECE[s], PIECE[s + 1]):
                            read_tile(v, k)
                    if s == 7:
                        normalise(u, 0)
                    if nxt2 and s == 9:
                        make_lo(v + 1)
                if nxt:
                    for k in range(PIECE[NS], NT):
                        read_tile(v, k)
                    both_parts(v)
                normalise(u, 1)
            units(dve, slot)


def output_block(nc, ps, io, scr):
    xt_d = io["xt"].rearrange("(o p) (c n) -> c p o n", p=P, n=CH)
    out_d = io["out"].rearrange("(o p) (c n) -> c p o n", p=P, n=CH)
    ctx = ExitStack()
    with ctx:
        sb = lambda name, shape, dt=F32: ctx.enter_context(nc.sbuf_tensor(name, shape, dt))
        sem = lambda name, ahead=0: Sem(ctx.enter_context(nc.semaphore(name)), ahead)
        ident = sb("o_ident", [P, P])
        wo = sb("wo_raw", [P, DC, D])
        wo_hi = sb("wo_hi", [P, DC, D], F32R)
        wo_lo = sb("wo_lo", [P, DC, D], F32R)
        heads = [sb(f"heads{i}", [P, TPC, D]) for i in range(2)]
        gate = [sb(f"gate{i}", [P, DC, CH]) for i in range(2)]
        xt = [sb(f"xt{i}", [P, DC, CH]) for i in range(2)]
        o_hi = [sb(f"o_hi{i}", [P, DC, CH], F32R) for i in range(2)]
        o_lo = [sb(f"o_lo{i}", [P, DC, CH], F32R) for i in range(2)]
        prod = sb("prod_sb", [P, DC, CH])
        res = [sb(f"res{i}", [P, DC, CH]) for i in range(2)]

        passed = sem("o_passed")
        consts, wo_in, wo_ok = sem("o_consts"), sem("wo_in"), sem("wo_ok")
        heads_in = [sem(f"heads_in{i}") for i in range(2)]
        more_in = [sem(f"more_in{i}") for i in range(2)]
        t_ok, hi_ok, lo_ok = sem("o_t_ok"), sem("o_hi_ok", 2), sem("o_lo_ok", 2)
        s_ok = sem("s_ok")
        gated = sem("gated", 1)
        res_ok = sem("res_ok", 2)
        res_out = [sem(f"res_out{i}", 16) for i in range(2)]
        block = ctx.enter_context(nc.Block())

        @block.sync
        def _(eng):
            for s in res_out:
                s.give(eng)
            eng.dma_start(wo[:, :, :], io["wo"].rearrange("(c p) n -> p c n", p=P)).then_inc(wo_in.handle, 16)
            def load(c, par):
                heads_in[par].by(eng.dma_start(heads[par][:, :, :], scr["heads"][c].rearrange("p t g n -> p t (g n)")), 16)
                more_in[par].by(eng.dma_start(gate[par][:, :, :], scr["gate"][c].rearrange("o p n -> p o n")), 16)
                more_in[par].by(eng.dma_start(xt[par][:, :, :], xt_d[c]), 16)

            load(0, 0)
            load(1, 1)
            with eng.Fori(0, NCHUNK // 2) as it:
                for par in range(2):
                    c = it * 2 + par
                    res_ok.wait_apart(eng, c + 1, passed)
                    res_out[par].by(eng.dma_start(out_d[c], res[par][:, :, :]), 16)
                    load((c + 2) % NCHUNK, par)
            for par in range(2):
                res_out[par].wait(eng, 16 * NCHUNK // 2)
                heads_in[par].wait(eng, 16 * (NCHUNK // 2 + 1))
                more_in[par].wait(eng, 32 * (NCHUNK // 2 + 1))

        @block.gpsimd
        def _(eng):
            consts.by(eng.memset(ident[:, :], 0.0))
            consts.wait(eng, 1)
            consts.by(eng.affine_select(out=ident[:, :], in_=ident[:, :], compare_op=ALU.not_equal, fill=1.0, base=0,
                                        pattern=[[-1, P]], channel_multiplier=1))

        @block.tensor
        def _(pe):
            consts.wait(pe, 2)
            wo_ok.wait(pe, 2)
            with pe.Fori(0, NCHUNK // 2) as it:
                for par in range(2):
                    c = it * 2 + par
                    heads_in[par].wait(pe, 16 * (it + 1))
                    hi_ok.wait(pe, c - 1)
                    lo_ok.wait(pe, c - 1)
                    for d in range(DC):
                        for t in range(TPC):
                            last = pe.transpose(ps[:, 2 * par + d, t * P:(t + 1) * P],
                                                heads[par][:, t, d * P:(d + 1) * P], ident[:, :])
                    t_ok.by(last)
                    hi_ok.wait(pe, c + 1)
                    lo_ok.wait(pe, c + 1)
                    gated.wait(pe, c)
                    for o in range(DC):
                        cols = slice(o * P, (o + 1) * P)
                        terms = [(w[:, d, cols], a[:, d, :]) for d in range(DC)
                                 for w, a in ((wo_hi, o_hi[par]), (wo_hi, o_lo[par]), (wo_lo, o_hi[par]))]
                        for n, (w, a) in enumerate(terms):
                            last = pe.matmul(ps[:, 4 + o, :], w, a, start=(n == 0), stop=(n == len(terms) - 1))
                    s_ok.by(last)

        @block.scalar
        def _(act):
            hi_ok.give(act)
            wo_in.wait(act, 16)
            wo_ok.by(act.copy(wo_hi[:, :, :], wo[:, :, :]))
            with act.Fori(0, NCHUNK // 2) as it:
                for par in range(2):
                    t_ok.wait(act, it * 2 + par + 1)
                    hi_ok.by(act.copy(o_hi[par][:, :, :], ps[:, 2 * par:2 * par + 2, :]))

        @block.vector
        def _(dve):
            for s in (lo_ok, gated, res_ok):
                s.give(dve)
            wo_ok.wait(dve, 1)
            wo_ok.by(dve.tensor_tensor(wo_lo[:, :, :], wo[:, :, :], wo_hi[:, :, :].bitcast(F32), op=ALU.subtract))
            with dve.Fori(0, NCHUNK // 2) as it:
                for par in range(2):
                    c = it * 2 + par
                    hi_ok.wait(dve, c + 1)
                    lo_ok.by(dve.tensor_tensor(o_lo[par][:, :, :], ps[:, 2 * par:2 * par + 2, :],
                                               o_hi[par][:, :, :].bitcast(F32), op=ALU.subtract))
                    s_ok.wait(dve, c + 1)
                    more_in[par].wait(dve, 32 * (it + 1))
                    gated.by(dve.tensor_tensor(prod[:, :, :], ps[:, 4:6, :], gate[par][:, :, :], op=ALU.mult))
                    gated.wait(dve, c + 1)
                    res_out[par].wait(dve, 16 * it)
                    res_ok.by(dve.tensor_tensor(res[par][:, :, :], prod[:, :, :], xt[par][:, :, :], op=ALU.add))


def build(nc, io):
    scr = {
        "qkv": nc.dram_tensor("scr_qkv", (B, NG, P, TB, 3 * HG * DH), F32).ap(),
        "gate": nc.dram_tensor("scr_gate", (NCHUNK, DC, P, CH), F32).ap(),
        "heads": nc.dram_tensor("scr_heads", (NCHUNK, P, TPC, NG, HG * DH), F32).ap(),
    }
    with nc.psum_tensor("ps", [P, 8, CH], F32) as ps:
        ffn_block(nc, ps, io, scr)
        attention_block(nc, ps, io, scr)
        output_block(nc, ps, io, scr)


def kernel(L0_attn_X, L0_attn_Wq, L0_attn_Wk, L0_attn_Wv, L0_attn_Wo, L0_ffn_SU_ug, L0_ffn_SU_dp,
           L0_ffn_Wscale_ug, L0_ffn_Wscale_dp, L0_ffn_W_up, L0_ffn_W_gate, L0_ffn_W_down):
    import numpy as np
    import concourse.bacc as bacc
    from concourse.bass_utils import run_bass_kernel_spmd

    lay = lambda a: np.ascontiguousarray(np.asarray(a))
    columns = lambda v: lay(np.asarray(v).reshape(-1, P).T)
    x = lay(L0_attn_X).reshape(NTOK, D)

    had = np.ones((1, 1), np.float32)
    while had.shape[0] < P:
        had = np.block([[had, had], [had, -had]])
    theta = np.float32(10000.0) ** (np.float32(-2.0) * np.arange(DH // 2, dtype=np.float32) / np.float32(DH))
    angles = np.arange(T, dtype=np.float32)[:, None] * theta[None, :].astype(np.float32)
    cos = np.repeat(np.cos(angles), 2, axis=1).astype(np.float32)
    sin = np.stack([-np.sin(angles), np.sin(angles)], axis=-1).reshape(T, DH).astype(np.float32)
    tokens = lambda a: lay(a.reshape(TB, P, DH).transpose(1, 0, 2))

    arrays = {
        "x": x,
        "xt": lay(x.T),
        "wqkv": lay(np.concatenate([np.asarray(w).T for w in (L0_attn_Wq, L0_attn_Wk, L0_attn_Wv)], axis=1)),
        "wo": lay(np.asarray(L0_attn_Wo).T),
        "wug": lay(np.concatenate([np.asarray(w).T for w in (L0_ffn_W_up, L0_ffn_W_gate)], axis=1)),
        "wd": lay(np.asarray(L0_ffn_W_down).T),
        "su_ug": columns(L0_ffn_SU_ug),
        "su_dp": columns(L0_ffn_SU_dp),
        "ws_ug": columns(L0_ffn_Wscale_ug),
        "ws_dp": columns(L0_ffn_Wscale_dp),
        "had": lay(had.astype(np.float32)),
        "cos": tokens(cos),
        "sin": tokens(sin),
    }
    nc = bacc.Bacc("TRN2", target_bir_lowering=False, num_devices=1)
    io = {n: nc.dram_tensor("in_" + n, a.shape, mybir.dt.from_np(a.dtype), kind="ExternalInput").ap()
          for n, a in arrays.items()}
    io["out"] = nc.dram_tensor("out_t", (D, NTOK), F32, kind="ExternalOutput").ap()
    build(nc, io)
    r = run_bass_kernel_spmd(nc, [{"in_" + n: a for n, a in arrays.items()}], core_ids=[0])
    return np.ascontiguousarray(r.results[0]["out_t"].T).reshape(B, T, D)
```

```python
import concourse.bass as bass
from concourse import mybir
from contextlib import ExitStack

F32 = mybir.dt.float32
F32R = mybir.dt.float32r
BF16 = mybir.dt.bfloat16
ALU = mybir.AluOpType
ACT = mybir.ActivationFunctionType
AX = mybir.AxisListType

P = 128
B, T, D, H, DH = 4, 1024, 256, 16, 16
INTER = 1024
SCALE = DH ** -0.5
EPS = 1e-5
CH = 512
NTOK = B * T
NCHUNK = NTOK // CH
TPC = CH // P
DC = D // P
IB = INTER // P
TB = T // P
HG = 4
NG = H // HG
NU = B * NG
NPAIR = HG // 2
SLOT = 64
NEG = -1.0e30


class Sem:

    def __init__(self, handle, ahead=0):
        self.handle, self.ahead = handle, ahead

    def wait(self, eng, count):
        eng.wait_ge(self.handle, count + self.ahead)

    def wait_apart(self, eng, count, passed):
        self.wait(eng, count)
        eng.sem_inc(passed.handle, 1)

    def by(self, ins, n=1):
        ins.then_inc(self.handle, n)
        return ins

    def give(self, eng):
        if self.ahead:
            eng.sem_inc(self.handle, self.ahead)


class Chain:

    def __init__(self, eng, handle):
        self.eng, self.handle, self.base, self.per, self.k, self.it = eng, handle, 0, 0, 0, 0

    def link(self, ins):
        ins.then_inc(self.handle, 1)
        self.k += 1
        self.eng.wait_ge(self.handle, self.it * self.per + (self.base + self.k))

    def link_apart(self, ins, passed):
        self.link(ins)
        self.eng.sem_inc(passed.handle, 1)

    def enter(self, it, per):
        self.it, self.per = it, per
        self.base += self.k
        self.k = 0

    def leave(self, iterations):
        assert self.k == self.per, (self.k, self.per)
        self.base += self.per * iterations
        self.it, self.per, self.k = 0, 0, 0


def ffn_block(nc, ps, io, scr):
    x_d = io["x"].rearrange("(c t p) d -> c p t d", t=TPC, p=P)
    ctx = ExitStack()
    with ctx:
        sb = lambda name, shape, dt=F32: ctx.enter_context(nc.sbuf_tensor(name, shape, dt))
        sem = lambda name, ahead=0: Sem(ctx.enter_context(nc.semaphore(name)), ahead)

        ident = sb("ident", [P, P])
        had = sb("had", [P, P])
        cos = sb("cos", [P, TB, DH])
        sin = sb("sin", [P, TB, DH])
        su_ug = sb("su_ug", [P, DC])
        su_dp = sb("su_dp", [P, IB])
        ws_ug = sb("ws_ug", [P, 2 * IB])
        ws_dp = sb("ws_dp", [P, DC])
        wqkv_hi = sb("wqkv_hi", [P, DC, 3 * D], F32R)
        wqkv_lo = sb("wqkv_lo", [P, DC, 3 * D], F32R)
        wug_hi = sb("wug_hi", [P, DC, 2 * INTER], F32R)
        wug_lo = sb("wug_lo", [P, DC, 2 * INTER], F32R)
        wd_hi = sb("wd_hi", [P, IB, D], F32R)
        wd_lo = sb("wd_lo", [P, IB, D], F32R)
        x_sb = sb("x_sb", [P, 2, TPC, D])
        xn = sb("xn", [P, TPC, D])
        stats = sb("stats", [P, TPC, 6])
        moments = sb("moments", [P, TPC, 2])
        var_eps = sb("var_eps", [P, TPC])
        minus_half = sb("minus_half", [P, TPC])
        rstd = sb("rstd", [P, TPC])
        xh = [sb(f"xh{i}", [P, DC, CH], F32R) for i in range(2)]
        xl = [sb(f"xl{i}", [P, DC, CH], F32R) for i in range(2)]
        y_sb = sb("y_sb", [P, 2, DC, CH])
        NHB = 4
        silu = sb("silu", [P, 2, CH])
        hid = sb("hid", [P, 2, CH])

        raw = ExitStack()
        rsb = lambda name, shape, dt=F32: raw.enter_context(nc.sbuf_tensor(name, shape, dt))
        with raw:
            prep_weights(nc, ps, io, rsb, ident, had, cos, sin, su_ug, su_dp, ws_ug, ws_dp,
                         wqkv_hi, wqkv_lo, wug_hi, wug_lo, wd_hi, wd_lo, minus_half)
        hid_hi = sb("hid_hi", [P, NHB, CH], F32R)
        hid_lo = sb("hid_lo", [P, NHB, CH], F32R)
        qkv = [sb(f"qkv{i}", [P, NG, TPC, 3 * HG * DH]) for i in range(2)]
        rot_a = sb("rot_a", [P, 2 * H, DH])
        rot_b = sb("rot_b", [P, 2 * H, DH])

        x_in = [sem(f"x_in{i}") for i in range(2)]
        var_ok = sem("var_ok")
        rstd_ok = sem("rstd_ok")
        xn_ok = sem("xn_ok")
        xt_ok = sem("xt_ok")
        xh_ok = sem("xh_ok")
        xl_ok = sem("xl_ok")
        qkv_ok = sem("qkv_ok")
        rot_read = sem("rot_read", 1)
        rot_ok = sem("rot_ok", 1)
        v_ok = sem("v_ok", 1)
        qkv_out = [sem(f"qkv_out{i}", 16) for i in range(2)]
        gu_ok = sem("gu_ok")
        silu_ok = sem("silu_ok")
        hid_ok = sem("hid_ok", 2)
        hh_ok = sem("hh_ok")
        hl_ok = sem("hl_ok")
        down_ok = sem("down_ok", NHB)
        y_ok = sem("y_ok", 1)
        y_out = [sem(f"y_out{i}", 16) for i in range(2)]
        passed = sem("passed")
        dve_chain = ctx.enter_context(nc.semaphore("dve_chain"))

        block = ctx.enter_context(nc.Block())

        def load_x(eng, c, par):
            eng.dma_start(x_sb[:, par], x_d[c]).then_inc(x_in[par].handle, 16)

        @block.sync
        def _(eng):
            for s in (*qkv_out, *y_out):
                s.give(eng)
            load_x(eng, 0, 0)
            load_x(eng, 1, 1)
            with eng.Fori(0, NCHUNK // 2) as it:
                for par in range(2):
                    c = it * 2 + par
                    xn_ok.wait_apart(eng, c + 1, passed)
                    load_x(eng, (c + 2) % NCHUNK, par)
                    rot_ok.wait_apart(eng, TPC * (c + 1), passed)
                    v_ok.wait_apart(eng, TPC * (c + 1), passed)
                    eng.dma_start(scr["qkv"][it, :, :, TPC * par:TPC * (par + 1), :].rearrange("g p t n -> p g t n"),
                                  qkv[par][:, :, :, :]).then_inc(qkv_out[par].handle, 16)
                    y_ok.wait_apart(eng, c + 1, passed)
                    eng.dma_start(scr["gate"][c].rearrange("o p n -> p o n"), y_sb[:, par]).then_inc(y_out[par].handle, 16)
            for par in range(2):
                qkv_out[par].wait(eng, 16 * NCHUNK // 2)
                y_out[par].wait(eng, 16 * NCHUNK // 2)
                x_in[par].wait(eng, 16 * (NCHUNK // 2 + 1))

        @block.gpsimd
        def _(eng):
            def rsqrt(n):
                var_ok.wait(eng, n)
                rstd_ok.by(eng.tensor_tensor(rstd[:, :], var_eps[:, :], minus_half[:, :], op=ALU.pow))
            rsqrt(1)
            with eng.Fori(0, NCHUNK) as c:
                rsqrt(c + 2)

        @block.tensor
        def _(pe):
            def transposes(n, par):
                xn_ok.wait(pe, n + 1)
                for d in range(DC):
                    for t in range(TPC):
                        last = pe.transpose(ps[:, 6 + d, t * P:(t + 1) * P], xn[:, t, d * P:(d + 1) * P], ident[:, :])
                xt_ok.by(last)

            def split_product(out, terms):
                for n, (lhs, rhs) in enumerate(terms):
                    last = pe.matmul(out, lhs, rhs, start=(n == 0), stop=(n == len(terms) - 1))
                return last

            def project(c, par, t):
                n = TPC * c + t
                rot_read.wait(pe, n)
                v_ok.wait(pe, n)
                tok = slice(t * P, (t + 1) * P)
                for bank, cols in ((6, slice(0, 2 * D)), (7, slice(2 * D, 3 * D))):
                    last = split_product(ps[:, bank, 0:cols.stop - cols.start],
                                         [(a[:, d, tok], w[:, d, cols]) for d in range(DC)
                                          for a, w in ((xh[par], wqkv_hi), (xh[par], wqkv_lo), (xl[par], wqkv_hi))])
                qkv_ok.by(last)

            def up_gate(c, par, ib):
                n = IB * c + ib
                hid_ok.wait(pe, n - 1)
                for k in range(2):
                    cols = slice(k * INTER + ib * P, k * INTER + (ib + 1) * P)
                    last = split_product(ps[:, 2 * (ib % 2) + k, :],
                                         [(w[:, d, cols], a[:, d, :]) for d in range(DC)
                                          for w, a in ((wug_hi, xh[par]), (wug_hi, xl[par]), (wug_lo, xh[par]))])
                gu_ok.by(last)

            def down(c, ib):
                n = IB * c + ib
                hh_ok.wait(pe, n + 1)
                hl_ok.wait(pe, n + 1)
                if ib == 0:
                    y_ok.wait(pe, c)
                r = ib % NHB
                for o in range(DC):
                    cols = slice(o * P, (o + 1) * P)
                    for k, (w, h) in enumerate(((wd_hi, hid_hi), (wd_hi, hid_lo), (wd_lo, hid_hi))):
                        last = pe.matmul(ps[:, 4 + o, :], w[:, ib, cols], h[:, r, :],
                                         start=(ib == 0 and k == 0), stop=(ib == IB - 1 and k == 2))
                down_ok.by(last)

            transposes(0, 0)
            with pe.Fori(0, NCHUNK // 2) as it:
                for par in range(2):
                    c = it * 2 + par
                    xh_ok.wait(pe, c + 1)
                    xl_ok.wait(pe, c + 1)
                    for ib in range(IB):
                        up_gate(c, par, ib)
                        if ib == 1:
                            project(c, par, 0)
                        if ib == 3:
                            project(c, par, 1)
                        if ib == 5:
                            rot_read.wait(pe, TPC * c + 2)
                            v_ok.wait(pe, TPC * c + 2)
                            transposes(c + 1, 1 - par)
                        if ib >= 2:
                            down(c, ib - 2)
                    xh_ok.wait(pe, c + 2)
                    xl_ok.wait(pe, c + 2)
                    project(c, par, 2)
                    down(c, IB - 2)
                    project(c, par, 3)
                    down(c, IB - 1)

        @block.scalar
        def _(act):
            v_ok.give(act)
            y_ok.give(act)

            def take_xh(n, par):
                xt_ok.wait(act, n + 1)
                xh_ok.by(act.copy(xh[par][:, :, :], ps[:, 6:8, :]))

            def take_v(c, par, t):
                qkv_ok.wait(act, TPC * c + t + 1)
                if t == 0:
                    qkv_out[par].wait(act, 8 * (c - par))
                v_ok.by(act.copy(qkv[par][:, :, t, 2 * HG * DH:],
                                 ps[:, 7, 0:D].rearrange("p (g n) -> p g n", g=NG)))

            take_xh(0, 0)
            with act.Fori(0, NCHUNK // 2) as it:
                for par in range(2):
                    c = it * 2 + par
                    for ib in range(IB):
                        n = IB * c + ib
                        gu_ok.wait(act, n + 1)
                        silu_ok.by(act.activation(silu[:, ib % 2, :], ps[:, 2 * (ib % 2) + 1, :], ACT.Silu,
                                                  scale=ws_ug[:, IB + ib:IB + ib + 1]))
                        hid_ok.wait(act, n + 1)
                        down_ok.wait(act, n - NHB + 1)
                        hh_ok.by(act.copy(hid_hi[:, ib % NHB, :], hid[:, ib % 2, :]))
                        if ib == 1:
                            take_v(c, par, 0)
                        if ib == 3:
                            take_v(c, par, 1)
                        if ib == 5:
                            take_xh(c + 1, 1 - par)
                    take_v(c, par, 2)
                    take_v(c, par, 3)
                    down_ok.wait(act, IB * (c + 1))
                    y_out[par].wait(act, 8 * (c - par))
                    for o in range(DC):
                        last = act.activation(y_sb[:, par, o, :], ps[:, 4 + o, :], ACT.Silu, scale=ws_dp[:, o:o + 1])
                    y_ok.by(last)

        @block.vector
        def _(dve):
            rot_read.give(dve)
            rot_ok.give(dve)
            hid_ok.give(dve)
            down_ok.give(dve)
            ch = Chain(dve, dve_chain)

            def layernorm(n, par, nth):
                x_in[par].wait(dve, 16 * (nth + 1))
                for t in range(TPC):
                    last = dve.bn_stats(stats[:, t, :], x_sb[:, par, t, :])
                ch.link_apart(last, passed)
                for t in range(TPC):
                    last = dve.bn_aggr(moments[:, t, :], stats[:, t, :])
                ch.link(last)
                var_ok.by(dve.tensor_scalar_add(var_eps[:, :], moments[:, :, 1], EPS))
                rstd_ok.wait(dve, n + 1)
                for t in range(TPC):
                    last = dve.tensor_scalar(xn[:, t, :], x_sb[:, par, t, :], moments[:, t, 0:1], rstd[:, t:t + 1],
                                             ALU.subtract, ALU.mult)
                xn_ok.by(last)

            def take_xl(n, par):
                xt_ok.wait(dve, n + 1)
                xh_ok.wait(dve, n + 1)
                xl_ok.by(dve.tensor_tensor(xl[par][:, :, :], ps[:, 6:8, :], xh[par][:, :, :].bitcast(F32), op=ALU.subtract))

            def rotate(c, par, t):
                tb = TPC * par + t
                qkv_ok.wait(dve, TPC * c + t + 1)
                src = ps[:, 6, :].rearrange("p (h d) -> p h d", d=DH)
                pairs = ps[:, 6, :].rearrange("p (h d two) -> p h d two", d=DH // 2, two=2)
                sins = sin[:, tb, :].rearrange("p (d two) -> p d two", two=2)
                b_out = rot_b[:, :, :].rearrange("p h (d two) -> p h d two", two=2)
                rot_ok.wait(dve, TPC * c + t)
                dve.tensor_tensor(rot_a[:, :, :], src, cos[:, tb:tb + 1, :].to_broadcast([P, 2 * H, DH]), op=ALU.mult)
                for k in range(2):
                    s = sins[:, :, k].rearrange("p (one d) -> p one d", one=1).to_broadcast([P, 2 * H, DH // 2])
                    last = dve.tensor_tensor(b_out[:, :, :, k], pairs[:, :, :, 1 - k], s, op=ALU.mult)
                rot_read.by(last)
                rot_read.wait(dve, TPC * c + t + 1)
                if t == 0:
                    qkv_out[par].wait(dve, 8 * (c - par))
                for k in range(2):
                    half = slice(k * H, (k + 1) * H)
                    dst = qkv[par][:, :, t, k * HG * DH:(k + 1) * HG * DH]
                    last = dve.tensor_tensor(dst,
                                             rot_a[:, half, :].rearrange("p (g h) d -> p g (h d)", g=NG),
                                             rot_b[:, half, :].rearrange("p (g h) d -> p g (h d)", g=NG), op=ALU.add)
                rot_ok.by(last)

            layernorm(0, 0, 0)
            take_xl(0, 0)
            with dve.Fori(0, NCHUNK // 2) as it:
                ch.enter(it, 4)
                for par in range(2):
                    c = it * 2 + par
                    for ib in range(IB):
                        n = IB * c + ib
                        gu_ok.wait(dve, n + 1)
                        silu_ok.wait(dve, n + 1)
                        hid_ok.by(dve.scalar_tensor_tensor(hid[:, ib % 2, :], ps[:, 2 * (ib % 2), :],
                                                           ws_ug[:, ib:ib + 1], silu[:, ib % 2, :], ALU.mult, ALU.mult))
                        hh_ok.wait(dve, n + 1)
                        hid_ok.wait(dve, n + 1)
                        hl_ok.by(dve.tensor_tensor(hid_lo[:, ib % NHB, :], hid[:, ib % 2, :],
                                                   hid_hi[:, ib % NHB, :].bitcast(F32), op=ALU.subtract))
                        if ib == 1:
                            rotate(c, par, 0)
                        if ib == 3:
                            rotate(c, par, 1)
                        if ib == 4:
                            layernorm(c + 1, 1 - par, it + par)
                        if ib == 5:
                            take_xl(c + 1, 1 - par)
                    rotate(c, par, 2)
                    rotate(c, par, 3)
            ch.leave(NCHUNK // 2)


def prep_weights(nc, ps, io, sb, ident, had, cos, sin, su_ug, su_dp, ws_ug, ws_dp,
                 wqkv_hi, wqkv_lo, wug_hi, wug_lo, wd_hi, wd_lo, minus_half):
    ctx = ExitStack()
    with ctx:
        sem = lambda name: Sem(ctx.enter_context(nc.semaphore(name)))
        wqkv = sb("wqkv_raw", [P, DC, 3 * D])
        wug = sb("wug_raw", [P, DC, 2 * INTER])
        wug_f = sb("wug_fold", [P, DC, 2 * INTER])
        wd = sb("wd_raw", [P, 2, IB, D])
        su_ug_s = sb("su_ug_s", [P, DC])
        su_dp_s = sb("su_dp_s", [P, IB])
        small_in, qkv_in, ug_in, d_in = sem("small_in"), sem("qkv_in"), sem("ug_in"), sem("d_in")
        ones_ok, ident_ok = sem("ones_ok"), sem("ident_ok")
        scale_ok = sem("scale_ok")
        ug_fold, d_fold = sem("ug_fold"), sem("d_fold")
        wq_hi = sem("wq_hi")
        prod, hi_ok, lo_ok = sem("prod"), sem("hi_ok"), sem("lo_ok")
        wq_lo = sem("wq_lo")
        NUG = DC * 2 * INTER // CH
        ND = IB * D // CH
        LOADS = 8
        block = ctx.enter_context(nc.Block())

        @block.sync
        def _(eng):
            eng.dma_start(wug[:, :, :], io["wug"].rearrange("(c p) n -> p c n", p=P)).then_inc(ug_in.handle, 16)
            eng.dma_start(wd[:, 0], io["wd"].rearrange("(c p) n -> p c n", p=P)).then_inc(d_in.handle, 16)

        @block.scalar
        def _(act):
            act.dma_start(wqkv[:, :, :], io["wqkv"].rearrange("(c p) n -> p c n", p=P)).then_inc(qkv_in.handle, 16)
            for dst, src in ((had, "had"), (cos, "cos"), (sin, "sin"), (su_ug, "su_ug"), (su_dp, "su_dp"),
                             (ws_ug, "ws_ug"), (ws_dp, "ws_dp")):
                full = tuple(slice(None) for _ in dst.shape)
                act.dma_start(dst[full], io[src]).then_inc(small_in.handle, 16)
            qkv_in.wait(act, 16)
            wq_hi.by(act.copy(wqkv_hi[:, :, :], wqkv[:, :, :]))
            scale_ok.wait(act, 2)
            for n in range(NUG + ND):
                prod.wait(act, n + 1)
                bank = ps[:, n % 8, :]
                if n < NUG:
                    o, cols = n // (NUG // DC), slice(n % (NUG // DC) * CH, (n % (NUG // DC) + 1) * CH)
                    last = act.mul(wug_hi[:, o, cols], bank, su_ug_s[:, o:o + 1])
                else:
                    for k in range(CH // D):
                        ib = (n - NUG) * (CH // D) + k
                        last = act.mul(wd_hi[:, ib, :], bank[:, k * D:(k + 1) * D], su_dp_s[:, ib:ib + 1])
                hi_ok.by(last)

        @block.gpsimd
        def _(eng):
            ones_ok.by(eng.memset(ident[:, :], 0.0))
            eng.memset(minus_half[:, :], -0.5)
            ones_ok.wait(eng, 1)
            ident_ok.by(eng.affine_select(out=ident[:, :], in_=ident[:, :], compare_op=ALU.not_equal, fill=1.0, base=0,
                                          pattern=[[-1, P]], channel_multiplier=1))

        @block.tensor
        def _(pe):
            small_in.wait(pe, 16 * 7)
            for n in range(NUG + ND):
                if n >= 8:
                    lo_ok.wait(pe, n - 7)
                if n < NUG:
                    o, k = n // (NUG // DC), n % (NUG // DC)
                    ug_fold.wait(pe, o + 1)
                    rhs = wug_f[:, o, k * CH:(k + 1) * CH]
                else:
                    d_fold.wait(pe, 3)
                    k = (n - NUG) * (CH // D)
                    rhs = wd[:, 1, k:k + CH // D, :]
                prod.by(pe.matmul(ps[:, n % 8, :], had[:, :], rhs, start=True, stop=True))

        @block.vector
        def _(dve):
            small_in.wait(dve, 16 * 7)
            scale_ok.by(dve.tensor_scalar_mul(su_ug_s[:, :], su_ug[:, :], float(D) ** -0.5))
            scale_ok.by(dve.tensor_scalar_mul(su_dp_s[:, :], su_dp[:, :], float(INTER) ** -0.5))
            ug_in.wait(dve, 16)
            for o, op in ((0, ALU.add), (1, ALU.subtract)):
                ug_fold.by(dve.tensor_tensor(wug_f[:, o, :], wug[:, 0, :], wug[:, 1, :], op=op))
            d_in.wait(dve, 16)
            for stage in range(3):
                step = 1 << stage
                if stage:
                    d_fold.wait(dve, stage)
                src, dst = (wd[:, i].rearrange("p (a two b) n -> p a two b n", two=2, b=step)
                            for i in (stage % 2, 1 - stage % 2))
                for o, op in ((0, ALU.add), (1, ALU.subtract)):
                    last = dve.tensor_tensor(dst[:, :, o], src[:, :, 0], src[:, :, 1], op=op)
                d_fold.by(last)
            wq_hi.wait(dve, 1)
            dve.tensor_tensor(wqkv_lo[:, :, :], wqkv[:, :, :], wqkv_hi[:, :, :].bitcast(F32), op=ALU.subtract)
            for n in range(NUG + ND):
                hi_ok.wait(dve, n + 1)
                bank = ps[:, n % 8, :]
                if n < NUG:
                    o, cols = n // (NUG // DC), slice(n % (NUG // DC) * CH, (n % (NUG // DC) + 1) * CH)
                    last = dve.scalar_tensor_tensor(wug_lo[:, o, cols], bank, su_ug_s[:, o:o + 1],
                                                    wug_hi[:, o, cols].bitcast(F32), ALU.mult, ALU.subtract)
                else:
                    for k in range(CH // D):
                        ib = (n - NUG) * (CH // D) + k
                        last = dve.scalar_tensor_tensor(wd_lo[:, ib, :], bank[:, k * D:(k + 1) * D],
                                                        su_dp_s[:, ib:ib + 1], wd_hi[:, ib, :].bitcast(F32),
                                                        ALU.mult, ALU.subtract)
                lo_ok.by(last)


def attention_block(nc, ps, io, scr):
    QC = T // CH
    STEPS = [(c, j) for c in range(QC) for j in range(TPC * (c + 1))]
    NS = len(STEPS)
    LAG = 2
    RING = 3
    first = lambda c, j: max(0, P * j - CH * c)
    diagonal = lambda c, j: P * j >= CH * c

    TILES = []
    for i in range(TB):
        for part in range(i // TPC + 1):
            w = min(P * (i + 1) - CH * part, CH)
            n = max(k for k in (1, 2, 4) if k * w <= CH)
            TILES += [(i, part, w, range(h, h + n)) for h in range(0, HG, n)]
    NT = len(TILES)
    A_TILES = sum(i < TPC for i, _, _, _ in TILES)
    assert NT % 2 == 0
    PER_STEP = [0, 3, 4, 4, 4, 4, 4, 4, 4, 3, 3, 1]
    FILLS = TB // 2
    PIECE = [sum(PER_STEP[:s]) for s in range(NS + 1)]

    ctx = ExitStack()
    with ctx:
        sb = lambda name, shape, dt=F32: ctx.enter_context(nc.sbuf_tensor(name, shape, dt))
        sem = lambda name, ahead=0: Sem(ctx.enter_context(nc.semaphore(name)), ahead)

        ident = sb("a_ident", [P, P])
        ident_b = sb("a_ident_b", [P, P], BF16)
        ident_r = sb("a_ident_r", [P, P], F32R)
        mask = sb("a_mask", [P, P], BF16)
        loaded = sb("loaded", [P, TB, 3 * HG * DH])
        slots = sb("slots", [P, TB, 2 * HG, SLOT], F32R)
        k_t = [sb(f"k_t{i}", [P, NPAIR, T], F32R) for i in range(2)]
        q_t = [sb(f"q_t{i}", [P, 2, NPAIR, T], F32R) for i in range(2)]
        v_ones = [sb(f"v_ones{i}", [P, TB, HG, 2 * DH]) for i in range(2)]
        probs = sb("probs", [P, RING, NPAIR, 2, CH])
        maxes = sb("maxes", [P, QC, TB, HG])
        maxes_b = sb("maxes_b", [P, TPC, HG])
        shift = [sb(f"shift{c}", [TPC * HG, P], F32R) for c in range(QC)]
        o_raw = [sb(f"o_raw{c}", [P, CH]) for c in range(QC)]
        o_inv = sb("o_inv", [P, QC, TPC, HG])
        o_nat = [sb(f"o_nat{c}", [P, TPC, HG * DH]) for c in range(QC)]

        passed = sem("a_passed")
        consts = sem("a_consts")
        zeros_ok = sem("zeros_ok")
        loaded_ok = sem("loaded_ok")
        hi_ok, lo_ok = sem("slots_hi"), sem("slots_lo")
        v_ok = sem("v_ones_ok")
        t_ok = sem("t_ok")
        t_act, t_dve = sem("t_act", 1), sem("t_dve", 1)
        tile_ok, tile_read = sem("tile_ok"), sem("tile_read", 2)
        maxb_ok = sem("maxb_ok")
        mt_ok, mt_read = sem("mt_ok"), sem("mt_read")
        row_in = [sem(f"row_in{c}", 64) for c in range(QC)]
        st_ok, exp_ok = sem("st_ok"), sem("exp_ok", 2)
        sel_ok = sem("sel_ok")
        pv_ok = sem("pv_ok", RING)
        o_read = sem("o_read", 1)
        ot_ok, o_ok = sem("ot_ok"), sem("o_ok", 1)
        inv_ok = sem("inv_ok")
        o_out = [sem(f"o_out{c}", 16) for c in range(QC)]
        S_BANK, PV_BANK, X_BANK = 0, 4, 7
        WORK = (5, 6, 7)
        turns, order = {}, []
        for s in range(NS):
            order += [("t", 2 * s), ("t", 2 * s + 1)] * (s < FILLS)
            order += [("m", k) for k in range(PIECE[s], PIECE[s + 1])]
        order += [("m", k) for k in range(PIECE[NS], NT)]
        for n, what in enumerate(order):
            turns[what] = WORK[n % len(WORK)]
        NDIAG = sum(diagonal(*s) for s in STEPS)

        block = ctx.enter_context(nc.Block())

        def units(eng, slot):
            with eng.Fori(0, NU // 2 - 1) as it:
                for par in range(2):
                    slot(it * 2 + par, par, True, True, it)
            slot(NU - 2, 0, True, False, NU // 2 - 1)
            slot(NU - 1, 1, False, False, NU // 2 - 1)

        @block.sync
        def _(eng):
            for s in (*row_in, *o_out):
                s.give(eng)

            def load(v, b, g):
                if not isinstance(v, int) or v > 0:
                    hi_ok.wait(eng, v)
                    lo_ok.wait(eng, v)
                    v_ok.wait_apart(eng, v, passed)
                loaded_ok.by(eng.dma_start(loaded[:, :, :], scr["qkv"][b, g]), 16)

            def rows(v, par, c):
                mt_read.wait(eng, QC * v + c + 1)
                for h in range(HG):
                    row = SLOT * (h % 2) + 2 * DH
                    row_in[c].by(eng.dma_start(q_t[par][row:row + 1, h % 2, h // 2, c * CH:(c + 1) * CH].bitcast(F32),
                                               shift[c][h:h + HG * (TPC - 1) + 1:HG, :].bitcast(F32)), 16)

            def store(u, c, b, g):
                o_ok.wait_apart(eng, QC * u + c + 1, passed)
                dst = scr["heads"][b * QC + c, :, :, g, :]
                o_out[c].by(eng.dma_start(dst, o_nat[c][:, :, :]), 16)

            load(0, 0, 0)
            load(1, 0, 1)
            rows(0, 0, 0)

            def slot(u, par, nxt, nxt2, it):
                b = it // 2 if isinstance(it, int) else it // 2
                g = (it % 2) * 2 + par
                rows(u, par, 1)
                if nxt2:
                    load(u + 2, (it + 1) // 2, ((it + 1) % 2) * 2 + par)
                if nxt:
                    rows(u + 1, 1 - par, 0)
                store(u, 0, b, g)
                store(u, 1, b, g)
            units(eng, slot)
            for c in range(QC):
                o_out[c].wait(eng, 16 * NU)

        @block.gpsimd
        def _(eng):
            consts.by(eng.memset(ident[:, :], 0.0))
            consts.by(eng.memset(mask[:, :], 0.0))
            for i in range(2):
                eng.memset(v_ones[i][:, :, :, DH:], 1.0)
            consts.by(eng.memset(slots[:, :, :, 2 * DH:3 * DH].bitcast(F32), 0.0))
            consts.wait(eng, 3)
            consts.by(eng.affine_select(out=ident[:, :], in_=ident[:, :], compare_op=ALU.not_equal, fill=1.0, base=0,
                                        pattern=[[-1, P]], channel_multiplier=1))
            consts.by(eng.affine_select(out=mask[:, :], in_=mask[:, :], compare_op=ALU.is_ge, fill=NEG, base=0,
                                        pattern=[[-1, P]], channel_multiplier=1))
            consts.by(eng.memset(slots[:, :, HG:, 2 * DH:2 * DH + 1].bitcast(F32), 1.0))
            consts.wait(eng, 6)
            eng.tensor_copy(ident_r[:, :], ident[:, :])
            consts.by(eng.tensor_copy(ident_b[:, :], ident[:, :]))

            def make_hi(v):
                loaded_ok.wait(eng, 16 * (v + 1))
                if not isinstance(v, int) or v > 0:
                    t_ok.wait_apart(eng, 2 * FILLS * v, passed)
                qk = loaded[:, :, 0:2 * HG * DH].rearrange("p t (h d) -> p t h d", d=DH)
                eng.tensor_copy(slots[:, :, :, 0:DH], qk)
                eng.tensor_copy(slots[:, :, 0:HG, DH:2 * DH], qk[:, :, 0:HG, :])
                hi_ok.by(eng.tensor_copy(slots[:, :, HG:, 3 * DH:], qk[:, :, HG:, :]))

            def take_v(v, par):
                src = loaded[:, :, 2 * HG * DH:].rearrange("p t (h d) -> p t h d", d=DH)
                v_ok.by(eng.tensor_copy(v_ones[par][:, :, :, 0:DH], src))

            make_hi(0)
            take_v(0, 0)
            make_hi(1)

            def slot(u, par, nxt, nxt2, it):
                for s, (c, j) in enumerate(STEPS):
                    if diagonal(c, j):
                        for p in range(NPAIR):
                            exp_ok.wait_apart(eng, NPAIR * (NS * u + s) + p + 1, passed)
                            r = (NS * par + s) % RING
                            v = probs[:, r, p, :, 0:P]
                            sel_ok.by(eng.affine_select(out=v, in_=v, compare_op=ALU.is_ge, fill=0.0, base=0,
                                                        pattern=[[0, 2], [1, P]], channel_multiplier=-1))
                    if s == TPC - 1:
                        if nxt:
                            take_v(u + 1, 1 - par)
                        if nxt2:
                            make_hi(u + 2)
            units(eng, slot)

        @block.tensor
        def _(pe):
            free = {bank: [] for bank in WORK}

            def claim(bank, reader, *more):
                waits = {}
                for s, base, n in (*free[bank], *more):
                    if s not in waits or waits[s][1] < n:
                        waits[s] = (base, n)
                for s, (base, n) in waits.items():
                    s.wait(pe, base + n)
                free[bank] = [reader]

            def to_rows(v, n):
                f, of_k = n // 2, n % 2
                bank = turns["t", n]
                more = [(hi_ok, v, 1), (lo_ok, v, 1)] if n == 0 else []
                claim(bank, (t_dve if of_k else t_act, FILLS * v, f + 1), *more)
                for p in range(NPAIR):
                    for t in range(2):
                        pair = slots[:, 2 * f + t, HG * of_k + 2 * p:HG * of_k + 2 * p + 2, :]
                        last = pe.transpose(ps[:, bank, (2 * p + t) * P:(2 * p + t + 1) * P].bitcast(F32R),
                                            pair.rearrange("p a b -> p (a b)"), ident_r[:, :])
                t_ok.by(last)

            def max_tile(v, par, k):
                i, part, w, heads = TILES[k]
                bank = turns["m", k]
                more = []
                if k == 0 or TILES[k - 1][0] < i:
                    more = [(t_act, FILLS * v, i // 2 + 1), (t_dve, FILLS * v, i // 2 + 1)]
                claim(bank, (tile_read, NT * v, k + 1), *more)
                for n, h in enumerate(heads):
                    masked = part == i // TPC
                    last = pe.matmul(ps[:, bank, n * w:(n + 1) * w], q_t[par][:, h % 2, h // 2, i * P:(i + 1) * P],
                                     k_t[par][:, h // 2, part * CH:part * CH + w], start=True, stop=not masked)
                    if masked:
                        last = pe.matmul(ps[:, bank, (n + 1) * w - P:(n + 1) * w], ident_b[:, :], mask[:, :],
                                         start=False, stop=True)
                tile_ok.by(last)

            def max_rows(v, c):
                found = (tile_read, NT * v, A_TILES) if c == 0 else (maxb_ok, v, 1)
                m = maxes[:, 0, 0:TPC, :] if c == 0 else maxes_b[:, :, :]
                claim(X_BANK, (mt_read, QC * v, c + 1), found)
                mt_ok.by(pe.transpose(ps[0:TPC * HG, X_BANK, 0:P], m.rearrange("p a b -> p (a b)"), ident[:, :]))

            def scores(u, par, s, p):
                c, j = STEPS[s]
                exp_ok.wait(pe, NPAIR * (NS * u + s - 1) + p + 1)
                if j == 0 and p == 0:
                    row_in[c].wait(pe, 16 * HG * (u + 1))
                q0 = CH * c + first(c, j)
                for e in range(2):
                    last = pe.matmul(ps[:, S_BANK + 2 * p + e, 0:CH - first(c, j)],
                                     k_t[par][:, p, j * P:(j + 1) * P],
                                     q_t[par][:, e, p, q0:(c + 1) * CH], start=True, stop=True)
                st_ok.by(last)

            def weigh(u, par, s):
                c, j = STEPS[s]
                exp_ok.wait(pe, NPAIR * (NS * u + s + 1))
                if diagonal(c, j):
                    d = sum(diagonal(*x) for x in STEPS[:s + 1])
                    sel_ok.wait(pe, NPAIR * (NDIAG * u + d))
                if s == 0:
                    v_ok.wait(pe, u + 1)
                if j == 0:
                    o_read.wait(pe, QC * u + c)
                r = (NS * par + s) % RING
                for h in range(HG):
                    last = pe.matmul(ps[2 * DH * h:2 * DH * (h + 1), PV_BANK, first(c, j):CH], v_ones[par][:, j, h, :],
                                     probs[:, r, h // 2, h % 2, 0:CH - first(c, j)],
                                     start=(j == 0), stop=(j == TPC * (c + 1) - 1))
                pv_ok.by(last)

            def to_tokens(u, c):
                claim(X_BANK, (o_ok, QC * u, c + 1), (o_read, QC * u, c + 1))
                for t in range(TPC):
                    last = pe.transpose(ps[:, X_BANK, t * P:(t + 1) * P], o_raw[c][:, t * P:(t + 1) * P], ident[:, :])
                ot_ok.by(last)

            consts.wait(pe, 7)
            zeros_ok.wait(pe, 1)
            for kind, n in order:
                to_rows(0, n) if kind == "t" else max_tile(0, 0, n)
                if (kind, n) == ("m", A_TILES + 3):
                    max_rows(0, 0)

            def slot(u, par, nxt, nxt2, it):
                v, vpar = u + 1, 1 - par
                for bank in WORK:
                    free[bank] = [(tile_read, NT * v, 0)]
                free[X_BANK] += [(o_ok, QC * u, 0), (mt_read, QC * u, 1)]
                for s in range(NS):
                    tiles = list(range(PIECE[s], PIECE[s + 1])) if nxt else []
                    if nxt and s < FILLS:
                        to_rows(v, 2 * s)
                        to_rows(v, 2 * s + 1)
                    scores(u, par, s, 0)
                    for k in tiles[:1]:
                        max_tile(v, vpar, k)
                    scores(u, par, s, 1)
                    for k in tiles[1:2]:
                        max_tile(v, vpar, k)
                    if s == 1:
                        max_rows(u, 1)
                    if s >= LAG:
                        weigh(u, par, s - LAG)
                    for k in tiles[2:]:
                        max_tile(v, vpar, k)
                    if nxt and s == 5:
                        max_rows(v, 0)
                    if s == 7:
                        to_tokens(u, 0)
                for s in range(NS - LAG, NS):
                    weigh(u, par, s)
                if nxt:
                    for k in range(PIECE[NS], NT):
                        max_tile(v, vpar, k)
                to_tokens(u, 1)
            units(pe, slot)

        @block.scalar
        def _(act):
            exp_ok.give(act)
            o_read.give(act)
            t_act.give(act)

            def take_q(v, par, f):
                t_ok.wait(act, 2 * FILLS * v + 2 * f + 1)
                for e in range(2):
                    half = slice(SLOT * e, SLOT * (e + 1))
                    last = act.copy(q_t[par][half, e, :, 2 * f * P:2 * (f + 1) * P],
                                    ps[half, turns["t", 2 * f], :].rearrange("p (x n) -> p x n", x=NPAIR))
                t_act.by(last)

            def take_max(v, c):
                mt_ok.wait(act, QC * v + c + 1)
                row_in[c].wait(act, 16 * HG * v)
                mt_read.by(act.mul(shift[c][:, :], ps[0:TPC * HG, X_BANK, 0:P], -1.0))

            def exponentials(u, par, s, p):
                c, j = STEPS[s]
                w = CH - first(c, j)
                st_ok.wait(act, NPAIR * (NS * u + s) + p + 1)
                pv_ok.wait(act, NS * u + s - RING + 1)
                bank = S_BANK + 2 * p
                exp_ok.by(act.activation(probs[:, (NS * par + s) % RING, p, :, 0:w], ps[:, bank:bank + 2, 0:w],
                                         ACT.Exp, scale=SCALE))

            def take_o(u, c):
                pv_ok.wait(act, NS * u + (TPC if c == 0 else NS))
                o_read.by(act.copy(o_raw[c][:, :], ps[:, PV_BANK, :]))

            for f in range(FILLS):
                take_q(0, 0, f)
            take_max(0, 0)

            def slot(u, par, nxt, nxt2, it):
                v, vpar = u + 1, 1 - par
                for s in range(NS):
                    if nxt and s < FILLS:
                        take_q(v, vpar, s)
                    exponentials(u, par, s, 0)
                    exponentials(u, par, s, 1)
                    if s == 1:
                        take_max(u, 1)
                    if nxt and s == 5:
                        take_max(v, 0)
                    if s == 5:
                        take_o(u, 0)
                take_o(u, 1)
            units(act, slot)

        @block.vector
        def _(dve):
            for s in (tile_read, pv_ok, t_dve, o_ok):
                s.give(dve)
            for i in range(2):
                for e in range(2):
                    last = dve.memset(q_t[i][SLOT * (1 - e):SLOT * (2 - e), e].bitcast(F32), 0.0)
            zeros_ok.by(last)

            def make_lo(v):
                hi_ok.wait(dve, v + 1)
                qk = loaded[:, :, 0:2 * HG * DH].rearrange("p t (h d) -> p t h d", d=DH)
                dve.tensor_tensor(slots[:, :, 0:HG, 3 * DH:], qk[:, :, 0:HG, :], slots[:, :, 0:HG, 0:DH].bitcast(F32),
                                  op=ALU.subtract)
                lo_ok.by(dve.tensor_tensor(slots[:, :, HG:, DH:2 * DH], qk[:, :, HG:, :],
                                           slots[:, :, HG:, 0:DH].bitcast(F32), op=ALU.subtract))

            def take_k(v, par, f):
                t_ok.wait(dve, 2 * FILLS * v + 2 * f + 2)
                t_dve.by(dve.tensor_copy(k_t[par][:, :, 2 * f * P:2 * (f + 1) * P],
                                         ps[:, turns["t", 2 * f + 1], :].rearrange("p (x n) -> p x n", x=NPAIR)))

            def read_tile(v, k):
                i, part, w, heads = TILES[k]
                tile_ok.wait(dve, NT * v + k + 1)
                n = len(heads)
                tile_read.by(dve.tensor_reduce(maxes[:, part, i, heads[0]:heads[-1] + 1],
                                               ps[:, turns["m", k], 0:n * w].rearrange("p (h k) -> p h k", h=n),
                                               axis=AX.X, op=ALU.max))

            def both_parts(v):
                tile_read.wait(dve, NT * (v + 1))
                maxb_ok.by(dve.tensor_tensor(maxes_b[:, :, :], maxes[:, 0, TPC:, :], maxes[:, 1, TPC:, :], op=ALU.max))

            def normalise(u, c):
                ot_ok.wait(dve, QC * u + c + 1)
                rows = ps[:, X_BANK, :].rearrange("p (t h d) -> p t h d", t=TPC, d=2 * DH)
                inv = o_inv[:, c]
                inv_ok.by(dve.reciprocal(inv, rows[:, :, :, DH]))
                inv_ok.wait(dve, QC * u + c + 1)
                o_out[c].wait(dve, 16 * u)
                o_ok.by(dve.tensor_tensor(o_nat[c][:, :, :].rearrange("p t (h d) -> p t h d", d=DH), rows[:, :, :, 0:DH],
                                          inv.rearrange("p t (h one) -> p t h one", one=1)
                                          .to_broadcast([P, TPC, HG, DH]), op=ALU.mult))

            make_lo(0)
            for kind, n in order:
                if kind == "m":
                    read_tile(0, n)
                elif n % 2:
                    take_k(0, 0, n // 2)
            both_parts(0)
            make_lo(1)

            def slot(u, par, nxt, nxt2, it):
                v = u + 1
                for s in range(NS):
                    if nxt and s < FILLS:
                        take_k(v, 1 - par, s)
                    if nxt:
                        for k in range(PIECE[s], PIECE[s + 1]):
                            read_tile(v, k)
                    if s == 7:
                        normalise(u, 0)
                    if nxt2 and s == 9:
                        make_lo(v + 1)
                if nxt:
                    for k in range(PIECE[NS], NT):
                        read_tile(v, k)
                    both_parts(v)
                normalise(u, 1)
            units(dve, slot)


def output_block(nc, ps, io, scr):
    xt_d = io["xt"].rearrange("(o p) (c n) -> c p o n", p=P, n=CH)
    out_d = io["out"].rearrange("(o p) (c n) -> c p o n", p=P, n=CH)
    ctx = ExitStack()
    with ctx:
        sb = lambda name, shape, dt=F32: ctx.enter_context(nc.sbuf_tensor(name, shape, dt))
        sem = lambda name, ahead=0: Sem(ctx.enter_context(nc.semaphore(name)), ahead)
        ident = sb("o_ident", [P, P])
        wo = sb("wo_raw", [P, DC, D])
        wo_hi = sb("wo_hi", [P, DC, D], F32R)
        wo_lo = sb("wo_lo", [P, DC, D], F32R)
        heads = [sb(f"heads{i}", [P, TPC, D]) for i in range(2)]
        gate = [sb(f"gate{i}", [P, DC, CH]) for i in range(2)]
        xt = [sb(f"xt{i}", [P, DC, CH]) for i in range(2)]
        o_hi = [sb(f"o_hi{i}", [P, DC, CH], F32R) for i in range(2)]
        o_lo = [sb(f"o_lo{i}", [P, DC, CH], F32R) for i in range(2)]
        prod = sb("prod_sb", [P, DC, CH])
        res = [sb(f"res{i}", [P, DC, CH]) for i in range(2)]

        passed = sem("o_passed")
        consts, wo_in, wo_ok = sem("o_consts"), sem("wo_in"), sem("wo_ok")
        heads_in = [sem(f"heads_in{i}") for i in range(2)]
        more_in = [sem(f"more_in{i}") for i in range(2)]
        t_ok, hi_ok, lo_ok = sem("o_t_ok"), sem("o_hi_ok", 2), sem("o_lo_ok", 2)
        s_ok = sem("s_ok")
        gated = sem("gated", 1)
        res_ok = sem("res_ok", 2)
        res_out = [sem(f"res_out{i}", 16) for i in range(2)]
        block = ctx.enter_context(nc.Block())

        @block.sync
        def _(eng):
            for s in res_out:
                s.give(eng)
            eng.dma_start(wo[:, :, :], io["wo"].rearrange("(c p) n -> p c n", p=P)).then_inc(wo_in.handle, 16)
            def load(c, par):
                heads_in[par].by(eng.dma_start(heads[par][:, :, :], scr["heads"][c].rearrange("p t g n -> p t (g n)")), 16)
                more_in[par].by(eng.dma_start(gate[par][:, :, :], scr["gate"][c].rearrange("o p n -> p o n")), 16)
                more_in[par].by(eng.dma_start(xt[par][:, :, :], xt_d[c]), 16)

            load(0, 0)
            load(1, 1)
            with eng.Fori(0, NCHUNK // 2) as it:
                for par in range(2):
                    c = it * 2 + par
                    res_ok.wait_apart(eng, c + 1, passed)
                    res_out[par].by(eng.dma_start(out_d[c], res[par][:, :, :]), 16)
                    load((c + 2) % NCHUNK, par)
            for par in range(2):
                res_out[par].wait(eng, 16 * NCHUNK // 2)
                heads_in[par].wait(eng, 16 * (NCHUNK // 2 + 1))
                more_in[par].wait(eng, 32 * (NCHUNK // 2 + 1))

        @block.gpsimd
        def _(eng):
            consts.by(eng.memset(ident[:, :], 0.0))
            consts.wait(eng, 1)
            consts.by(eng.affine_select(out=ident[:, :], in_=ident[:, :], compare_op=ALU.not_equal, fill=1.0, base=0,
                                        pattern=[[-1, P]], channel_multiplier=1))

        @block.tensor
        def _(pe):
            consts.wait(pe, 2)
            wo_ok.wait(pe, 2)
            with pe.Fori(0, NCHUNK // 2) as it:
                for par in range(2):
                    c = it * 2 + par
                    heads_in[par].wait(pe, 16 * (it + 1))
                    hi_ok.wait(pe, c - 1)
                    lo_ok.wait(pe, c - 1)
                    for d in range(DC):
                        for t in range(TPC):
                            last = pe.transpose(ps[:, 2 * par + d, t * P:(t + 1) * P],
                                                heads[par][:, t, d * P:(d + 1) * P], ident[:, :])
                    t_ok.by(last)
                    hi_ok.wait(pe, c + 1)
                    lo_ok.wait(pe, c + 1)
                    gated.wait(pe, c)
                    for o in range(DC):
                        cols = slice(o * P, (o + 1) * P)
                        terms = [(w[:, d, cols], a[:, d, :]) for d in range(DC)
                                 for w, a in ((wo_hi, o_hi[par]), (wo_hi, o_lo[par]), (wo_lo, o_hi[par]))]
                        for n, (w, a) in enumerate(terms):
                            last = pe.matmul(ps[:, 4 + o, :], w, a, start=(n == 0), stop=(n == len(terms) - 1))
                    s_ok.by(last)

        @block.scalar
        def _(act):
            hi_ok.give(act)
            wo_in.wait(act, 16)
            wo_ok.by(act.copy(wo_hi[:, :, :], wo[:, :, :]))
            with act.Fori(0, NCHUNK // 2) as it:
                for par in range(2):
                    t_ok.wait(act, it * 2 + par + 1)
                    hi_ok.by(act.copy(o_hi[par][:, :, :], ps[:, 2 * par:2 * par + 2, :]))

        @block.vector
        def _(dve):
            for s in (lo_ok, gated, res_ok):
                s.give(dve)
            wo_ok.wait(dve, 1)
            wo_ok.by(dve.tensor_tensor(wo_lo[:, :, :], wo[:, :, :], wo_hi[:, :, :].bitcast(F32), op=ALU.subtract))
            with dve.Fori(0, NCHUNK // 2) as it:
                for par in range(2):
                    c = it * 2 + par
                    hi_ok.wait(dve, c + 1)
                    lo_ok.by(dve.tensor_tensor(o_lo[par][:, :, :], ps[:, 2 * par:2 * par + 2, :],
                                               o_hi[par][:, :, :].bitcast(F32), op=ALU.subtract))
                    s_ok.wait(dve, c + 1)
                    more_in[par].wait(dve, 32 * (it + 1))
                    gated.by(dve.tensor_tensor(prod[:, :, :], ps[:, 4:6, :], gate[par][:, :, :], op=ALU.mult))
                    gated.wait(dve, c + 1)
                    res_out[par].wait(dve, 16 * it)
                    res_ok.by(dve.tensor_tensor(res[par][:, :, :], prod[:, :, :], xt[par][:, :, :], op=ALU.add))


def build(nc, io):
    scr = {
        "qkv": nc.dram_tensor("scr_qkv", (B, NG, P, TB, 3 * HG * DH), F32).ap(),
        "gate": nc.dram_tensor("scr_gate", (NCHUNK, DC, P, CH), F32).ap(),
        "heads": nc.dram_tensor("scr_heads", (NCHUNK, P, TPC, NG, HG * DH), F32).ap(),
    }
    with nc.psum_tensor("ps", [P, 8, CH], F32) as ps:
        ffn_block(nc, ps, io, scr)
        attention_block(nc, ps, io, scr)
        output_block(nc, ps, io, scr)


def kernel(L0_attn_X, L0_attn_Wq, L0_attn_Wk, L0_attn_Wv, L0_attn_Wo, L0_ffn_SU_ug, L0_ffn_SU_dp,
           L0_ffn_Wscale_ug, L0_ffn_Wscale_dp, L0_ffn_W_up, L0_ffn_W_gate, L0_ffn_W_down):
    import numpy as np
    import concourse.bacc as bacc
    from concourse.bass_utils import run_bass_kernel_spmd

    lay = lambda a: np.ascontiguousarray(np.asarray(a))
    columns = lambda v: lay(np.asarray(v).reshape(-1, P).T)
    x = lay(L0_attn_X).reshape(NTOK, D)

    had = np.ones((1, 1), np.float32)
    while had.shape[0] < P:
        had = np.block([[had, had], [had, -had]])
    theta = np.float32(10000.0) ** (np.float32(-2.0) * np.arange(DH // 2, dtype=np.float32) / np.float32(DH))
    angles = np.arange(T, dtype=np.float32)[:, None] * theta[None, :].astype(np.float32)
    cos = np.repeat(np.cos(angles), 2, axis=1).astype(np.float32)
    sin = np.stack([-np.sin(angles), np.sin(angles)], axis=-1).reshape(T, DH).astype(np.float32)
    tokens = lambda a: lay(a.reshape(TB, P, DH).transpose(1, 0, 2))

    arrays = {
        "x": x,
        "xt": lay(x.T),
        "wqkv": lay(np.concatenate([np.asarray(w).T for w in (L0_attn_Wq, L0_attn_Wk, L0_attn_Wv)], axis=1)),
        "wo": lay(np.asarray(L0_attn_Wo).T),
        "wug": lay(np.concatenate([np.asarray(w).T for w in (L0_ffn_W_up, L0_ffn_W_gate)], axis=1)),
        "wd": lay(np.asarray(L0_ffn_W_down).T),
        "su_ug": columns(L0_ffn_SU_ug),
        "su_dp": columns(L0_ffn_SU_dp),
        "ws_ug": columns(L0_ffn_Wscale_ug),
        "ws_dp": columns(L0_ffn_Wscale_dp),
        "had": lay(had.astype(np.float32)),
        "cos": tokens(cos),
        "sin": tokens(sin),
    }
    nc = bacc.Bacc("TRN2", target_bir_lowering=False, num_devices=1)
    io = {n: nc.dram_tensor("in_" + n, a.shape, mybir.dt.from_np(a.dtype), kind="ExternalInput").ap()
          for n, a in arrays.items()}
    io["out"] = nc.dram_tensor("out_t", (D, NTOK), F32, kind="ExternalOutput").ap()
    build(nc, io)
    r = run_bass_kernel_spmd(nc, [{"in_" + n: a for n, a in arrays.items()}], core_ids=[0])
    return np.ascontiguousarray(r.results[0]["out_t"].T).reshape(B, T, D)
```

```python
import concourse.bass as bass
from concourse import mybir
from contextlib import ExitStack

F32 = mybir.dt.float32
F32R = mybir.dt.float32r
BF16 = mybir.dt.bfloat16
ALU = mybir.AluOpType
ACT = mybir.ActivationFunctionType
AX = mybir.AxisListType

P = 128
B, T, D, H, DH = 4, 1024, 256, 16, 16
INTER = 1024
SCALE = DH ** -0.5
EPS = 1e-5
CH = 512
NTOK = B * T
NCHUNK = NTOK // CH
TPC = CH // P
DC = D // P
IB = INTER // P
TB = T // P
HG = 4
NG = H // HG
NU = B * NG
NPAIR = HG // 2
SLOT = 64
NEG = -1.0e30


class Sem:

    def __init__(self, handle, ahead=0):
        self.handle, self.ahead = handle, ahead

    def wait(self, eng, count):
        eng.wait_ge(self.handle, count + self.ahead)

    def wait_apart(self, eng, count, passed):
        self.wait(eng, count)
        eng.sem_inc(passed.handle, 1)

    def by(self, ins, n=1):
        ins.then_inc(self.handle, n)
        return ins

    def give(self, eng):
        if self.ahead:
            eng.sem_inc(self.handle, self.ahead)


class Chain:

    def __init__(self, eng, handle):
        self.eng, self.handle, self.base, self.per, self.k, self.it = eng, handle, 0, 0, 0, 0

    def link(self, ins):
        ins.then_inc(self.handle, 1)
        self.k += 1
        self.eng.wait_ge(self.handle, self.it * self.per + (self.base + self.k))

    def link_apart(self, ins, passed):
        self.link(ins)
        self.eng.sem_inc(passed.handle, 1)

    def enter(self, it, per):
        self.it, self.per = it, per
        self.base += self.k
        self.k = 0

    def leave(self, iterations):
        assert self.k == self.per, (self.k, self.per)
        self.base += self.per * iterations
        self.it, self.per, self.k = 0, 0, 0


class SlotOperands:

    def __init__(self, nc, ctx, scr):
        sb = lambda name, shape, dt=F32: ctx.enter_context(nc.sbuf_tensor(name, shape, dt))
        sem = lambda name, ahead=0: Sem(ctx.enter_context(nc.semaphore(name)), ahead)
        self.ident = sb("ident", [P, P])
        self.ident_b = sb("ident_b", [P, P], BF16)
        self.ident_r = sb("ident_r", [P, P], F32R)
        self.mask = sb("mask", [P, HG, P], BF16)
        self.loaded = sb("loaded", [P, TB, 3 * HG * DH])
        self.slots = sb("slots", [P, TB, 2 * HG, SLOT], F32R)
        self.q_t = sb("q_t0", [P, 2, NPAIR, T], F32R)
        self.qkv_d = scr["qkv"]
        self.loaded_ok = sem("loaded_ok")
        self.hi_ok, self.lo_ok = sem("slots_hi"), sem("slots_lo")
        self.qkv_out = [sem(f"qkv_out{i}", 16) for i in range(2)]
        self.y_out = [sem(f"y_out{i}", 16) for i in range(2)]

    def constants(self, eng, done):
        done.by(eng.memset(self.mask[:, :, :], 0.0))
        done.by(eng.memset(self.slots[:, :, :, 2 * DH:3 * DH].bitcast(F32), 0.0))
        done.wait(eng, 2)
        for e in range(2):
            done.by(eng.memset(self.q_t[SLOT * (1 - e):SLOT * (2 - e), e].bitcast(F32), 0.0))
            done.wait(eng, 3 + e)
        eng.affine_select(out=self.mask[:, :, :], in_=self.mask[:, :, :], compare_op=ALU.is_ge, fill=NEG, base=0,
                          pattern=[[0, HG], [-1, P]], channel_multiplier=1)
        eng.memset(self.slots[:, :, HG:, 2 * DH:2 * DH + 1].bitcast(F32), 1.0)
        eng.tensor_copy(self.ident_r[:, :], self.ident[:, :])
        eng.tensor_copy(self.ident_b[:, :], self.ident[:, :])

    def load(self, eng, b, g):
        self.loaded_ok.by(eng.dma_start(self.loaded[:, :, :], self.qkv_d[b, g]), 16)

    def split_hi(self, eng):
        qk = self.loaded[:, :, 0:2 * HG * DH].rearrange("p t (h d) -> p t h d", d=DH)
        eng.tensor_copy(self.slots[:, :, :, 0:DH], qk)
        eng.tensor_copy(self.slots[:, :, 0:HG, DH:2 * DH], qk[:, :, 0:HG, :])
        self.hi_ok.by(eng.tensor_copy(self.slots[:, :, HG:, 3 * DH:], qk[:, :, HG:, :]))

    def split_lo(self, eng, v):
        self.hi_ok.wait(eng, v + 1)
        qk = self.loaded[:, :, 0:2 * HG * DH].rearrange("p t (h d) -> p t h d", d=DH)
        eng.tensor_tensor(self.slots[:, :, 0:HG, 3 * DH:], qk[:, :, 0:HG, :],
                          self.slots[:, :, 0:HG, 0:DH].bitcast(F32), op=ALU.subtract)
        self.lo_ok.by(eng.tensor_tensor(self.slots[:, :, HG:, DH:2 * DH], qk[:, :, HG:, :],
                                        self.slots[:, :, HG:, 0:DH].bitcast(F32), op=ALU.subtract))


def ffn_block(nc, ps, io, scr, first_unit):
    x_d = io["x"].rearrange("(c t p) d -> c p t d", t=TPC, p=P)
    ctx = ExitStack()
    with ctx:
        sb = lambda name, shape, dt=F32: ctx.enter_context(nc.sbuf_tensor(name, shape, dt))
        sem = lambda name, ahead=0: Sem(ctx.enter_context(nc.semaphore(name)), ahead)

        ident = first_unit.ident
        had = sb("had", [P, P])
        cos_sin = sb("cos_sin", [P, 2, TB, DH])
        cos, sin = cos_sin[:, 0], cos_sin[:, 1]
        scales = sb("scales", [P, DC + IB + 2 * IB + DC])
        su_ug, su_dp = scales[:, 0:DC], scales[:, DC:DC + IB]
        ws_ug, ws_dp = scales[:, DC + IB:DC + 3 * IB], scales[:, DC + 3 * IB:]
        wqkv_hi = sb("wqkv_hi", [P, DC, 3 * D], F32R)
        wqkv_lo = sb("wqkv_lo", [P, DC, 3 * D], F32R)
        wug_hi = sb("wug_hi", [P, DC, 2 * INTER], F32R)
        wug_lo = sb("wug_lo", [P, DC, 2 * INTER], F32R)
        wd_hi = sb("wd_hi", [P, IB, D], F32R)
        wd_lo = sb("wd_lo", [P, IB, D], F32R)
        x_sb = sb("x_sb", [P, 2, TPC, D])
        xn = sb("xn", [P, TPC, D])
        stats = sb("stats", [P, TPC, 6])
        moments = sb("moments", [P, TPC, 2])
        var_eps = sb("var_eps", [P, TPC])
        minus_half = sb("minus_half", [P, TPC])
        rstd = sb("rstd", [P, TPC])
        xh = [sb(f"xh{i}", [P, DC, CH], F32R) for i in range(2)]
        xl = [sb(f"xl{i}", [P, DC, CH], F32R) for i in range(2)]
        y_sb = sb("y_sb", [P, 2, DC, CH])
        NHB = 4
        silu = sb("silu", [P, 2, CH])
        hid = sb("hid", [P, 2, CH])

        x_in = [sem(f"x_in{i}") for i in range(2)]
        var_ok = sem("var_ok")
        rstd_ok = sem("rstd_ok")
        xn_ok = sem("xn_ok")
        xt_ok = sem("xt_ok")
        xh_ok = sem("xh_ok")
        xl_ok = sem("xl_ok")
        passed = sem("passed")
        dve_chain = ctx.enter_context(nc.semaphore("dve_chain"))

        def load_x(eng, c, par):
            eng.dma_start(x_sb[:, par], x_d[c]).then_inc(x_in[par].handle, 16)

        def rsqrt(eng, n):
            var_ok.wait(eng, n)
            rstd_ok.by(eng.tensor_tensor(rstd[:, :], var_eps[:, :], minus_half[:, :], op=ALU.pow))

        def transposes(pe, n, par):
            xn_ok.wait(pe, n + 1)
            for d in range(DC):
                for t in range(TPC):
                    last = pe.transpose(ps[:, 6 + d, t * P:(t + 1) * P], xn[:, t, d * P:(d + 1) * P], ident[:, :])
            xt_ok.by(last)

        def take_xh(act, n, par):
            xt_ok.wait(act, n + 1)
            xh_ok.by(act.copy(xh[par][:, :, :], ps[:, 6:8, :]))

        def variances(dve, ch, n, par, nth):
            x_in[par].wait(dve, 16 * (nth + 1))
            for t in range(TPC):
                last = dve.bn_stats(stats[:, t, :], x_sb[:, par, t, :])
            ch.link_apart(last, passed)
            for t in range(TPC):
                last = dve.bn_aggr(moments[:, t, :], stats[:, t, :])
            ch.link(last)
            var_ok.by(dve.tensor_scalar_add(var_eps[:, :], moments[:, :, 1], EPS))

        def normalise(dve, n, par):
            rstd_ok.wait(dve, n + 1)
            for t in range(TPC):
                last = dve.tensor_scalar(xn[:, t, :], x_sb[:, par, t, :], moments[:, t, 0:1], rstd[:, t:t + 1],
                                         ALU.subtract, ALU.mult)
            xn_ok.by(last)

        def take_xl(dve, n, par):
            xt_ok.wait(dve, n + 1)
            xh_ok.wait(dve, n + 1)
            xl_ok.by(dve.tensor_tensor(xl[par][:, :, :], ps[:, 6:8, :], xh[par][:, :, :].bitcast(F32), op=ALU.subtract))

        def first_chunk(what, eng):
            if what == "load":
                load_x(eng, 0, 0)
            elif what == "rsqrt":
                rsqrt(eng, 1)
            elif what == "normalise":
                ch = Chain(eng, dve_chain)
                variances(eng, ch, 0, 0, 0)
                normalise(eng, 0, 0)
            elif what == "transposes":
                transposes(eng, 0, 0)
            elif what == "hi":
                take_xh(eng, 0, 0)
            elif what == "lo":
                take_xl(eng, 0, 0)

        raw = ExitStack()
        rsb = lambda name, shape, dt=F32: raw.enter_context(nc.sbuf_tensor(name, shape, dt))
        with raw:
            prep_weights(nc, ps, io, rsb, ident, had, cos_sin, scales, su_ug, su_dp,
                         wqkv_hi, wqkv_lo, wug_hi, wug_lo, wd_hi, wd_lo, minus_half, first_chunk)
        hid_hi = sb("hid_hi", [P, NHB, CH], F32R)
        hid_lo = sb("hid_lo", [P, NHB, CH], F32R)
        qkv = [sb(f"qkv{i}", [P, NG, TPC, 3 * HG * DH]) for i in range(2)]
        rot_a = sb("rot_a", [P, 2 * H, DH])
        rot_b = sb("rot_b", [P, 2 * H, DH])

        pool_consts = sem("pool_consts")
        qkv_ok = sem("qkv_ok")
        rot_read = sem("rot_read", 1)
        rot_ok = sem("rot_ok", 1)
        v_ok = sem("v_ok", 1)
        qkv_out, y_out = first_unit.qkv_out, first_unit.y_out
        gu_ok = sem("gu_ok")
        silu_ok = sem("silu_ok")
        hid_ok = sem("hid_ok", 2)
        hh_ok = sem("hh_ok")
        hl_ok = sem("hl_ok")
        down_ok = sem("down_ok", NHB)
        y_ok = sem("y_ok", 1)

        block = ctx.enter_context(nc.Block())

        @block.sync
        def _(eng):
            for s in (*qkv_out, *y_out):
                s.give(eng)
            load_x(eng, 1, 1)

            def pair(it):
                for par in range(2):
                    c = it * 2 + par
                    xn_ok.wait_apart(eng, c + 1, passed)
                    load_x(eng, (c + 2) % NCHUNK, par)
                    for tiles in (range(0, TPC - 1), range(TPC - 1, TPC)):
                        rot_ok.wait_apart(eng, TPC * c + tiles.stop, passed)
                        v_ok.wait_apart(eng, TPC * c + tiles.stop, passed)
                        dst = scr["qkv"][it, :, :, TPC * par + tiles.start:TPC * par + tiles.stop, :]
                        qkv_out[par].by(eng.dma_start(dst.rearrange("g p t n -> p g t n"),
                                                      qkv[par][:, :, tiles.start:tiles.stop, :]), 16)
                    y_ok.wait_apart(eng, c + 1, passed)
                    eng.dma_start(scr["gate"][c].rearrange("o p n -> p o n"), y_sb[:, par]).then_inc(y_out[par].handle, 16)
            with eng.Fori(0, NCHUNK // 2 - 1) as it:
                pair(it)
            for par in range(2):
                qkv_out[par].wait(eng, 32)
            first_unit.load(eng, 0, 0)
            pair(NCHUNK // 2 - 1)
            for par in range(2):
                qkv_out[par].wait(eng, 32 * NCHUNK // 2)
                y_out[par].wait(eng, 16 * NCHUNK // 2)
                x_in[par].wait(eng, 16 * (NCHUNK // 2 + 1))

        @block.gpsimd
        def _(eng):
            first_unit.constants(eng, pool_consts)
            with eng.Fori(0, NCHUNK) as c:
                rsqrt(eng, c + 2)
            first_unit.loaded_ok.wait(eng, 16)
            first_unit.split_hi(eng)

        @block.tensor
        def _(pe):
            def split_product(out, terms):
                for n, (lhs, rhs) in enumerate(terms):
                    last = pe.matmul(out, lhs, rhs, start=(n == 0), stop=(n == len(terms) - 1))
                return last

            def project(c, par, t):
                n = TPC * c + t
                rot_read.wait(pe, n)
                v_ok.wait(pe, n)
                tok = slice(t * P, (t + 1) * P)
                for bank, cols in ((6, slice(0, 2 * D)), (7, slice(2 * D, 3 * D))):
                    last = split_product(ps[:, bank, 0:cols.stop - cols.start],
                                         [(a[:, d, tok], w[:, d, cols]) for d in range(DC)
                                          for a, w in ((xh[par], wqkv_hi), (xh[par], wqkv_lo), (xl[par], wqkv_hi))])
                qkv_ok.by(last)

            def up_gate(c, par, ib):
                n = IB * c + ib
                hid_ok.wait(pe, n - 1)
                for k in range(2):
                    cols = slice(k * INTER + ib * P, k * INTER + (ib + 1) * P)
                    last = split_product(ps[:, 2 * (ib % 2) + k, :],
                                         [(w[:, d, cols], a[:, d, :]) for d in range(DC)
                                          for w, a in ((wug_hi, xh[par]), (wug_hi, xl[par]), (wug_lo, xh[par]))])
                gu_ok.by(last)

            def down(c, ib):
                n = IB * c + ib
                hh_ok.wait(pe, n + 1)
                hl_ok.wait(pe, n + 1)
                if ib == 0:
                    y_ok.wait(pe, c)
                r = ib % NHB
                for o in range(DC):
                    cols = slice(o * P, (o + 1) * P)
                    for k, (w, h) in enumerate(((wd_hi, hid_hi), (wd_hi, hid_lo), (wd_lo, hid_hi))):
                        last = pe.matmul(ps[:, 4 + o, :], w[:, ib, cols], h[:, r, :],
                                         start=(ib == 0 and k == 0), stop=(ib == IB - 1 and k == 2))
                down_ok.by(last)

            with pe.Fori(0, NCHUNK // 2) as it:
                for par in range(2):
                    c = it * 2 + par
                    xh_ok.wait(pe, c + 1)
                    xl_ok.wait(pe, c + 1)
                    for ib in range(IB):
                        up_gate(c, par, ib)
                        if ib == 1:
                            project(c, par, 0)
                        if ib == 3:
                            project(c, par, 1)
                        if ib == 5:
                            rot_read.wait(pe, TPC * c + 2)
                            v_ok.wait(pe, TPC * c + 2)
                            transposes(pe, c + 1, 1 - par)
                        if ib >= 2:
                            down(c, ib - 2)
                    xh_ok.wait(pe, c + 2)
                    xl_ok.wait(pe, c + 2)
                    project(c, par, 2)
                    down(c, IB - 2)
                    project(c, par, 3)
                    down(c, IB - 1)

        @block.scalar
        def _(act):
            v_ok.give(act)
            y_ok.give(act)

            def take_v(c, par, t):
                qkv_ok.wait(act, TPC * c + t + 1)
                if t == 0:
                    qkv_out[par].wait(act, 16 * (c - par))
                v_ok.by(act.copy(qkv[par][:, :, t, 2 * HG * DH:],
                                 ps[:, 7, 0:D].rearrange("p (g n) -> p g n", g=NG)))

            with act.Fori(0, NCHUNK // 2) as it:
                for par in range(2):
                    c = it * 2 + par
                    for ib in range(IB):
                        n = IB * c + ib
                        gu_ok.wait(act, n + 1)
                        silu_ok.by(act.activation(silu[:, ib % 2, :], ps[:, 2 * (ib % 2) + 1, :], ACT.Silu,
                                                  scale=ws_ug[:, IB + ib:IB + ib + 1]))
                        hid_ok.wait(act, n + 1)
                        down_ok.wait(act, n - NHB + 1)
                        hh_ok.by(act.copy(hid_hi[:, ib % NHB, :], hid[:, ib % 2, :]))
                        if ib == 1:
                            take_v(c, par, 0)
                        if ib == 3:
                            take_v(c, par, 1)
                        if ib == 5:
                            take_xh(act, c + 1, 1 - par)
                    take_v(c, par, 2)
                    take_v(c, par, 3)
                    down_ok.wait(act, IB * (c + 1))
                    y_out[par].wait(act, 8 * (c - par))
                    for o in range(DC):
                        last = act.activation(y_sb[:, par, o, :], ps[:, 4 + o, :], ACT.Silu, scale=ws_dp[:, o:o + 1])
                    y_ok.by(last)

        @block.vector
        def _(dve):
            rot_read.give(dve)
            rot_ok.give(dve)
            hid_ok.give(dve)
            down_ok.give(dve)
            ch = Chain(dve, dve_chain)
            ch.base = 2
            def rotate(c, par, t):
                tb = TPC * par + t
                qkv_ok.wait(dve, TPC * c + t + 1)
                src = ps[:, 6, :].rearrange("p (h d) -> p h d", d=DH)
                pairs = ps[:, 6, :].rearrange("p (h d two) -> p h d two", d=DH // 2, two=2)
                sins = sin[:, tb, :].rearrange("p (d two) -> p d two", two=2)
                b_out = rot_b[:, :, :].rearrange("p h (d two) -> p h d two", two=2)
                rot_ok.wait(dve, TPC * c + t)
                dve.tensor_tensor(rot_a[:, :, :], src, cos[:, tb:tb + 1, :].to_broadcast([P, 2 * H, DH]), op=ALU.mult)
                for k in range(2):
                    s = sins[:, :, k].rearrange("p (one d) -> p one d", one=1).to_broadcast([P, 2 * H, DH // 2])
                    last = dve.tensor_tensor(b_out[:, :, :, k], pairs[:, :, :, 1 - k], s, op=ALU.mult)
                rot_read.by(last)
                rot_read.wait(dve, TPC * c + t + 1)
                if t == 0:
                    qkv_out[par].wait(dve, 16 * (c - par))
                for k in range(2):
                    half = slice(k * H, (k + 1) * H)
                    dst = qkv[par][:, :, t, k * HG * DH:(k + 1) * HG * DH]
                    last = dve.tensor_tensor(dst,
                                             rot_a[:, half, :].rearrange("p (g h) d -> p g (h d)", g=NG),
                                             rot_b[:, half, :].rearrange("p (g h) d -> p g (h d)", g=NG), op=ALU.add)
                rot_ok.by(last)

            with dve.Fori(0, NCHUNK // 2) as it:
                ch.enter(it, 4)
                for par in range(2):
                    c = it * 2 + par
                    for ib in range(IB):
                        n = IB * c + ib
                        gu_ok.wait(dve, n + 1)
                        silu_ok.wait(dve, n + 1)
                        hid_ok.by(dve.scalar_tensor_tensor(hid[:, ib % 2, :], ps[:, 2 * (ib % 2), :],
                                                           ws_ug[:, ib:ib + 1], silu[:, ib % 2, :], ALU.mult, ALU.mult))
                        hh_ok.wait(dve, n + 1)
                        hid_ok.wait(dve, n + 1)
                        hl_ok.by(dve.tensor_tensor(hid_lo[:, ib % NHB, :], hid[:, ib % 2, :],
                                                   hid_hi[:, ib % NHB, :].bitcast(F32), op=ALU.subtract))
                        if ib == 1:
                            rotate(c, par, 0)
                        if ib == 2:
                            variances(dve, ch, c + 1, 1 - par, it + par)
                        if ib == 3:
                            rotate(c, par, 1)
                            normalise(dve, c + 1, 1 - par)
                        if ib == 5:
                            take_xl(dve, c + 1, 1 - par)
                    rotate(c, par, 2)
                    rotate(c, par, 3)
            ch.leave(NCHUNK // 2)
            first_unit.split_lo(dve, 0)


def prep_weights(nc, ps, io, sb, ident, had, cos_sin, scales, su_ug, su_dp,
                 wqkv_hi, wqkv_lo, wug_hi, wug_lo, wd_hi, wd_lo, minus_half, first_chunk):
    ctx = ExitStack()
    with ctx:
        sem = lambda name: Sem(ctx.enter_context(nc.semaphore(name)))
        wqkv = sb("wqkv_raw", [P, DC, 3 * D])
        wug = sb("wug_raw", [P, DC, 2 * INTER])
        wug_f = sb("wug_fold", [P, DC, 2 * INTER])
        wd = sb("wd_raw", [P, 2, IB, D])
        su_ug_s = sb("su_ug_s", [P, DC])
        su_dp_s = sb("su_dp_s", [P, IB])
        small_in, qkv_in, d_in = sem("small_in"), sem("qkv_in"), sem("d_in")
        late_in = sem("late_in")
        PARTS = 4
        ug_in = [sem(f"ug_in{i}") for i in range(PARTS)]
        ones_ok, ident_ok = sem("ones_ok"), sem("ident_ok")
        scale_ok = sem("scale_ok")
        ug_fold, d_fold = sem("ug_fold"), sem("d_fold")
        wq_hi = sem("wq_hi")
        prod, hi_ok, lo_ok = sem("prod"), sem("hi_ok"), sem("lo_ok")
        NUG = DC * 2 * INTER // CH
        ND = IB * D // CH
        BANKS = 6
        PART = 2 * INTER // PARTS
        UG = [(o, k) for i in range(PARTS) for o in range(DC) for k in range(i * PART // CH, (i + 1) * PART // CH)]
        block = ctx.enter_context(nc.Block())

        @block.sync
        def _(eng):
            small_in.by(eng.dma_start(had[:, :], io["had"]), 16)
            small_in.by(eng.dma_start(scales[:, :], io["scales"]), 16)
            src = io["wug"].rearrange("(c p) n -> p c n", p=P)
            for i in range(PARTS):
                cols = slice(i * PART, (i + 1) * PART)
                ug_in[i].by(eng.dma_start(wug[:, :, cols], src[:, :, cols]), 16)
            first_chunk("load", eng)
            qkv_in.by(eng.dma_start(wqkv[:, :, :], io["wqkv"].rearrange("(c p) n -> p c n", p=P)), 16)
            late_in.by(eng.dma_start(cos_sin[:, :, :, :], io["cos_sin"]), 16)
            late_in.wait(eng, 16)

        @block.scalar
        def _(act):
            d_in.by(act.dma_start(wd[:, 0], io["wd"].rearrange("(c p) n -> p c n", p=P)), 16)
            scale_ok.wait(act, 2)
            for n in range(NUG + ND):
                if n == NUG:
                    qkv_in.wait(act, 16)
                    wq_hi.by(act.copy(wqkv_hi[:, :, :], wqkv[:, :, :]))
                    first_chunk("hi", act)
                prod.wait(act, n + 1)
                bank = ps[:, n % BANKS, :]
                if n < NUG:
                    o, cols = UG[n][0], slice(UG[n][1] * CH, (UG[n][1] + 1) * CH)
                    last = act.mul(wug_hi[:, o, cols], bank, su_ug_s[:, o:o + 1])
                else:
                    for k in range(CH // D):
                        ib = (n - NUG) * (CH // D) + k
                        last = act.mul(wd_hi[:, ib, :], bank[:, k * D:(k + 1) * D], su_dp_s[:, ib:ib + 1])
                hi_ok.by(last)

        @block.gpsimd
        def _(eng):
            ones_ok.by(eng.memset(ident[:, :], 0.0))
            eng.memset(minus_half[:, :], -0.5)
            ones_ok.wait(eng, 1)
            ident_ok.by(eng.affine_select(out=ident[:, :], in_=ident[:, :], compare_op=ALU.not_equal, fill=1.0, base=0,
                                          pattern=[[-1, P]], channel_multiplier=1))
            d_in.wait(eng, 16)
            for stage in range(3):
                step = 1 << stage
                if stage:
                    d_fold.wait(eng, stage)
                src, dst = (wd[:, i].rearrange("p (a two b) n -> p a two b n", two=2, b=step)
                            for i in (stage % 2, 1 - stage % 2))
                for o, op in ((0, ALU.add), (1, ALU.subtract)):
                    last = eng.tensor_tensor(dst[:, :, o], src[:, :, 0], src[:, :, 1], op=op)
                d_fold.by(last)
                if stage == 1:
                    first_chunk("rsqrt", eng)

        @block.tensor
        def _(pe):
            small_in.wait(pe, 16 * 2)
            for n in range(NUG + ND):
                if n == NUG:
                    ident_ok.wait(pe, 1)
                    first_chunk("transposes", pe)
                if n >= BANKS:
                    lo_ok.wait(pe, n - BANKS + 1)
                if n < NUG:
                    o, k = UG[n]
                    ug_fold.wait(pe, n // (PART // CH) + 1)
                    rhs = wug_f[:, o, k * CH:(k + 1) * CH]
                else:
                    d_fold.wait(pe, 3)
                    k = (n - NUG) * (CH // D)
                    rhs = wd[:, 1, k:k + CH // D, :]
                prod.by(pe.matmul(ps[:, n % BANKS, :], had[:, :], rhs, start=True, stop=True))

        @block.vector
        def _(dve):
            small_in.wait(dve, 16 * 2)
            scale_ok.by(dve.tensor_scalar_mul(su_ug_s[:, :], su_ug[:, :], float(D) ** -0.5))
            scale_ok.by(dve.tensor_scalar_mul(su_dp_s[:, :], su_dp[:, :], float(INTER) ** -0.5))
            for i in range(PARTS):
                ug_in[i].wait(dve, 16)
                cols = slice(i * PART, (i + 1) * PART)
                for o, op in ((0, ALU.add), (1, ALU.subtract)):
                    ug_fold.by(dve.tensor_tensor(wug_f[:, o, cols], wug[:, 0, cols], wug[:, 1, cols], op=op))
            for n in range(NUG + ND):
                if n == NUG:
                    wq_hi.wait(dve, 1)
                    dve.tensor_tensor(wqkv_lo[:, :, :], wqkv[:, :, :], wqkv_hi[:, :, :].bitcast(F32), op=ALU.subtract)
                    first_chunk("lo", dve)
                hi_ok.wait(dve, n + 1)
                bank = ps[:, n % BANKS, :]
                if n == NUG // 2:
                    first_chunk("normalise", dve)
                if n < NUG:
                    o, cols = UG[n][0], slice(UG[n][1] * CH, (UG[n][1] + 1) * CH)
                    last = dve.scalar_tensor_tensor(wug_lo[:, o, cols], bank, su_ug_s[:, o:o + 1],
                                                    wug_hi[:, o, cols].bitcast(F32), ALU.mult, ALU.subtract)
                else:
                    for k in range(CH // D):
                        ib = (n - NUG) * (CH // D) + k
                        last = dve.scalar_tensor_tensor(wd_lo[:, ib, :], bank[:, k * D:(k + 1) * D],
                                                        su_dp_s[:, ib:ib + 1], wd_hi[:, ib, :].bitcast(F32),
                                                        ALU.mult, ALU.subtract)
                lo_ok.by(last)


class OutputOperands:
    RING = 4

    def __init__(self, nc, ctx, io, scr):
        sb = lambda name, shape, dt=F32: ctx.enter_context(nc.sbuf_tensor(name, shape, dt))
        sem = lambda name, ahead=0: Sem(ctx.enter_context(nc.semaphore(name)), ahead)
        self.heads = sb("heads_in", [P, self.RING, TPC, D])
        self.gate = sb("gate_in", [P, NCHUNK, DC, CH])
        self.xt = sb("xt_in", [P, NCHUNK, DC, CH])
        self.o_nat = [sb(f"o_nat{c}", [P, TPC, HG * DH]) for c in range(T // CH)]
        self.wo = sb("wo_raw", [P, DC, D])
        self.wo_hi = sb("wo_hi", [P, DC, D], F32R)
        self.wo_lo = sb("wo_lo", [P, DC, D], F32R)
        self.o_out = [sem(f"o_out{c}", 16) for c in range(T // CH)]
        self.wo_in, self.wo_ok = sem("wo_in"), sem("wo_ok")
        self.heads_in = [sem(f"heads_in{r}") for r in range(self.RING)]
        self.more_in = sem("more_in")
        self.heads_d, self.gate_d, self.wo_d = scr["heads"], scr["gate"], io["wo"].rearrange("(c p) n -> p c n", p=P)
        self.xt_d = io["xt"].rearrange("(o p) (c n) -> c p o n", p=P, n=CH)

    def load_heads(self, eng, c, r):
        self.heads_in[r].by(eng.dma_start(self.heads[:, r], self.heads_d[c].rearrange("p t g n -> p t (g n)")), 16)

    def load_more(self, eng, c):
        self.more_in.by(eng.dma_start(self.gate[:, c], self.gate_d[c].rearrange("o p n -> p o n")), 16)
        self.more_in.by(eng.dma_start(self.xt[:, c], self.xt_d[c]), 16)


def attention_block(nc, ps, scr, first_unit, shared):
    QC = T // CH
    STEPS = [(c, j) for c in range(QC) for j in range(TPC * (c + 1))]
    NS = len(STEPS)
    LAG = 2
    RING = 3
    first = lambda c, j: max(0, P * j - CH * c)
    diagonal = lambda c, j: P * j >= CH * c

    TILES = []
    for i in range(TB):
        for part in range(i // TPC + 1):
            w = min(P * (i + 1) - CH * part, CH)
            n = max(k for k in (1, 2, 4) if k * w <= CH)
            TILES += [(i, part, w, range(h, h + n)) for h in range(0, HG, n)]
    NT = len(TILES)
    A_TILES = sum(i < TPC for i, _, _, _ in TILES)
    PER_STEP = [0, 3, 5, 5, 4, 4, 4, 4, 4, 3, 1, 1]
    FILLS = TB // 2
    ACT_TAKES_K = {1}
    by_act = lambda n: (n % 2 == 0) != (n // 2 in ACT_TAKES_K)
    assert sum(PER_STEP) == NT
    PIECE = [sum(PER_STEP[:s]) for s in range(NS + 1)]
    HEAD = LAG

    ctx = ExitStack()
    with ctx:
        sb = lambda name, shape, dt=F32: ctx.enter_context(nc.sbuf_tensor(name, shape, dt))
        sem = lambda name, ahead=0: Sem(ctx.enter_context(nc.semaphore(name)), ahead)

        ident, ident_b, ident_r, mask = first_unit.ident, first_unit.ident_b, first_unit.ident_r, first_unit.mask
        loaded, slots = first_unit.loaded, first_unit.slots
        loaded_ok, hi_ok, lo_ok = first_unit.loaded_ok, first_unit.hi_ok, first_unit.lo_ok
        k_t = [sb(f"k_t{i}", [P, NPAIR, T], F32R) for i in range(2)]
        q_t = [first_unit.q_t, sb("q_t1", [P, 2, NPAIR, T], F32R)]
        v_ones = [sb(f"v_ones{i}", [P, TB, HG, 2 * DH]) for i in range(2)]
        probs = sb("probs", [P, RING, NPAIR, 2, CH])
        maxes = sb("maxes", [P, QC, TB, HG])
        maxes_b = sb("maxes_b", [P, TPC, HG])
        shift = [sb(f"shift{c}", [TPC * HG, P], F32R) for c in range(QC)]
        o_raw = [sb(f"o_raw{c}", [P, CH]) for c in range(QC)]
        o_inv = sb("o_inv", [P, QC, TPC, HG])
        o_nat = shared.o_nat

        passed = sem("a_passed")
        zeros_ok = sem("zeros_ok")
        v_ok = sem("v_ones_ok")
        t_ok = sem("t_ok")
        t_act, t_dve = sem("t_act", 1), sem("t_dve", 1)
        tile_ok, tile_read = sem("tile_ok"), sem("tile_read", 2)
        maxb_ok = sem("maxb_ok")
        mt_ok, mt_read = sem("mt_ok"), sem("mt_read")
        row_in = [sem(f"row_in{c}", 64) for c in range(QC)]
        st_ok, exp_ok = sem("st_ok"), sem("exp_ok", 2)
        sel_ok = sem("sel_ok")
        pv_ok = sem("pv_ok", RING)
        o_read = sem("o_read", 1)
        ot_ok, o_ok = sem("ot_ok"), sem("o_ok", 1)
        inv_ok = sem("inv_ok")
        o_out = shared.o_out
        S_BANK, PV_BANK = 0, 4
        WORK = (5, 6, 7)
        order = []
        for s in range(NS):
            order += [(s, "t", 2 * s), (s, "t", 2 * s + 1)] * (s < FILLS)
            tiles = [(s, "m", k) for k in range(PIECE[s], PIECE[s + 1])]
            order += tiles[:2] + [(s, "r", 1)] * (s == 1) + tiles[2:]
            order += [(s, "r", 0)] * (s == 5) + [(s, "o", 0)] * (s == 7) + [(s, "o", 1)] * (s == 1)
        turns = {what[1:]: WORK[n % len(WORK)] for n, what in enumerate(order)}
        NDIAG = sum(diagonal(*s) for s in STEPS)

        block = ctx.enter_context(nc.Block())

        def units(eng, step, window=lambda u, par, it, nxt: None, end=lambda: None):
            for s in range(HEAD):
                step(0, 0, s, True, True, False)

            def steps(u, par, it, left):
                window(u, par, it, left > 0)
                for s in range(HEAD, NS):
                    step(u, par, s, left > 0, left > 1, True)
                if left > 0:
                    for s in range(HEAD):
                        step(u + 1, 1 - par, s, left > 1, left > 2, True)

            with eng.Fori(0, NU // 2 - 1) as it:
                for par in range(2):
                    steps(it * 2 + par, par, it, 3)
            steps(NU - 2, 0, NU // 2 - 1, 1)
            steps(NU - 1, 1, NU // 2 - 1, 0)
            end()

        def take(eng, copy, v, par, n):
            f, cols = n // 2, slice(n // 2 * 2 * P, (n // 2 + 1) * 2 * P)
            t_ok.wait(eng, 2 * FILLS * v + n + 1)
            if n % 2:
                last = copy(k_t[par][:, :, cols], ps[:, turns["t", n], :].rearrange("p (x n) -> p x n", x=NPAIR))
            else:
                for e in range(2):
                    half = slice(SLOT * e, SLOT * (e + 1))
                    last = copy(q_t[par][half, e, :, cols],
                                ps[half, turns["t", n], :].rearrange("p (x n) -> p x n", x=NPAIR))
            (t_act if by_act(n) else t_dve).by(last)

        def takes(of_act, f):
            return [n for n in (2 * f, 2 * f + 1) if by_act(n) == of_act]

        @block.sync
        def _(eng):
            for s in (*row_in, *o_out):
                s.give(eng)

            def load(v, b, g):
                if not isinstance(v, int) or v > 0:
                    hi_ok.wait(eng, v)
                    lo_ok.wait(eng, v)
                    v_ok.wait_apart(eng, v, passed)
                first_unit.load(eng, b, g)

            def rows(v, par, c):
                mt_read.wait(eng, QC * v + c + 1)
                for h in range(HG):
                    row = SLOT * (h % 2) + 2 * DH
                    row_in[c].by(eng.dma_start(q_t[par][row:row + 1, h % 2, h // 2, c * CH:(c + 1) * CH].bitcast(F32),
                                               shift[c][h:h + HG * (TPC - 1) + 1:HG, :].bitcast(F32)), 16)

            def store(u, c, b, g):
                o_ok.wait_apart(eng, QC * u + c + 1, passed)
                dst = scr["heads"][b * QC + c, :, :, g, :]
                o_out[c].by(eng.dma_start(dst, o_nat[c][:, :, :]), 16)

            load(1, 0, 1)
            shared.wo_in.by(eng.dma_start(shared.wo[:, :, :], shared.wo_d), 16)
            rows(0, 0, 0)
            rows(0, 0, 1)

            def window(u, par, it, nxt):
                if not isinstance(u, int):
                    load(u + 2, (it + 1) // 2, ((it + 1) % 2) * 2 + par)
                    if par == 0:
                        shared.load_more(eng, it)
                else:
                    if par == 0:
                        shared.load_more(eng, it)
                    for r in range(RING // 2 * par, RING // 2 * (par + 1)):
                        o_out[r % QC].wait(eng, 16 * NG * (r // QC + 1))
                        shared.load_heads(eng, r, r)
                g = (it % 2) * 2 + par
                for c in range(QC):
                    if nxt:
                        rows(u + 1, 1 - par, c)
                    store(u, c, it // 2, g)
            RING = shared.RING
            units(eng, lambda *a: None, window)

        @block.gpsimd
        def _(eng):
            def make_hi(v):
                loaded_ok.wait(eng, 16 * (v + 1))
                t_ok.wait_apart(eng, 2 * FILLS * v, passed)
                first_unit.split_hi(eng)

            def take_v(v, par):
                src = loaded[:, :, 2 * HG * DH:].rearrange("p t (h d) -> p t h d", d=DH)
                v_ok.by(eng.tensor_copy(v_ones[par][:, :, :, 0:DH], src))

            for i in range(2):
                eng.memset(v_ones[i][:, :, :, DH:], 1.0)
            take_v(0, 0)
            v_ok.wait(eng, 1)
            for e in range(2):
                zeros_ok.by(eng.memset(q_t[1][SLOT * (1 - e):SLOT * (2 - e), e].bitcast(F32), 0.0))
            zeros_ok.wait(eng, 2)
            make_hi(1)

            def step(u, par, s, nxt, nxt2, prev):
                if diagonal(*STEPS[s]):
                    for p in range(NPAIR):
                        exp_ok.wait_apart(eng, NPAIR * (NS * u + s) + p + 1, passed)
                        v = probs[:, (NS * par + s) % RING, p, :, 0:P]
                        sel_ok.by(eng.affine_select(out=v, in_=v, compare_op=ALU.is_ge, fill=0.0, base=0,
                                                    pattern=[[0, 2], [1, P]], channel_multiplier=-1))
                if s == TPC - 1:
                    if nxt:
                        take_v(u + 1, 1 - par)
                    if nxt2:
                        make_hi(u + 2)
            units(eng, step)

        @block.tensor
        def _(pe):
            free = {bank: [] for bank in WORK}

            def claim(bank, reader, *more):
                waits = {}
                for s, base, n in (*free[bank], *more):
                    if s not in waits or waits[s][1] < n:
                        waits[s] = (base, n)
                for s, (base, n) in waits.items():
                    s.wait(pe, base + n)
                free[bank] = [reader]

            def to_rows(v, n):
                f, of_k = n // 2, n % 2
                bank = turns["t", n]
                more = [(hi_ok, v, 1), (lo_ok, v, 1)] if n == 0 else []
                claim(bank, (t_act if by_act(n) else t_dve, FILLS * v, f + 1), *more)
                for p in range(NPAIR):
                    for t in range(2):
                        pair = slots[:, 2 * f + t, HG * of_k + 2 * p:HG * of_k + 2 * p + 2, :]
                        last = pe.transpose(ps[:, bank, (2 * p + t) * P:(2 * p + t + 1) * P].bitcast(F32R),
                                            pair.rearrange("p a b -> p (a b)"), ident_r[:, :])
                t_ok.by(last)

            def max_tile(v, par, k):
                i, part, w, heads = TILES[k]
                bank = turns["m", k]
                more = []
                if k == 0 or TILES[k - 1][0] < i:
                    more = [(t_act, FILLS * v, i // 2 + 1), (t_dve, FILLS * v, i // 2 + 1)]
                claim(bank, (tile_read, NT * v, k + 1), *more)
                masked = part == i // TPC
                if w == P:
                    pe.matmul(ps[:, bank, 0:len(heads) * w], ident_b[:, :], mask[:, 0:len(heads), :],
                              start=True, stop=False)
                for n, h in enumerate(heads):
                    alone = not masked or (w == P and n == len(heads) - 1)
                    last = pe.matmul(ps[:, bank, n * w:(n + 1) * w], q_t[par][:, h % 2, h // 2, i * P:(i + 1) * P],
                                     k_t[par][:, h // 2, part * CH:part * CH + w], start=w > P, stop=alone)
                    if masked and w > P:
                        last = pe.matmul(ps[:, bank, (n + 1) * w - P:(n + 1) * w], ident_b[:, :], mask[:, 0, :],
                                         start=False, stop=True)
                tile_ok.by(last)

            def max_rows(v, c):
                found = (tile_read, NT * v, A_TILES) if c == 0 else (maxb_ok, v, 1)
                m = maxes[:, 0, 0:TPC, :] if c == 0 else maxes_b[:, :, :]
                bank = turns["r", c]
                claim(bank, (mt_read, QC * v, c + 1), found)
                mt_ok.by(pe.transpose(ps[0:TPC * HG, bank, 0:P], m.rearrange("p a b -> p (a b)"), ident[:, :]))

            def scores(u, par, s, p):
                c, j = STEPS[s]
                exp_ok.wait(pe, NPAIR * (NS * u + s - 1) + p + 1)
                if j == 0 and p == 0:
                    row_in[c].wait(pe, 16 * HG * (u + 1))
                q0 = CH * c + first(c, j)
                for e in range(2):
                    last = pe.matmul(ps[:, S_BANK + 2 * p + e, 0:CH - first(c, j)],
                                     k_t[par][:, p, j * P:(j + 1) * P],
                                     q_t[par][:, e, p, q0:(c + 1) * CH], start=True, stop=True)
                st_ok.by(last)

            def weigh(u, par, s):
                c, j = STEPS[s]
                exp_ok.wait(pe, NPAIR * (NS * u + s + 1))
                if diagonal(c, j):
                    d = sum(diagonal(*x) for x in STEPS[:s + 1])
                    sel_ok.wait(pe, NPAIR * (NDIAG * u + d))
                if s == 0:
                    v_ok.wait(pe, u + 1)
                if j == 0:
                    o_read.wait(pe, QC * u + c)
                r = (NS * par + s) % RING
                for h in range(HG):
                    last = pe.matmul(ps[2 * DH * h:2 * DH * (h + 1), PV_BANK, first(c, j):CH], v_ones[par][:, j, h, :],
                                     probs[:, r, h // 2, h % 2, 0:CH - first(c, j)],
                                     start=(j == 0), stop=(j == TPC * (c + 1) - 1))
                pv_ok.by(last)

            def to_tokens(u, c):
                bank = turns["o", c]
                claim(bank, (o_ok, QC * u, c + 1), (o_read, QC * u, c + 1))
                for t in range(TPC):
                    last = pe.transpose(ps[:, bank, t * P:(t + 1) * P], o_raw[c][:, t * P:(t + 1) * P], ident[:, :])
                ot_ok.by(last)

            for _, kind, n in order:
                if kind == "t":
                    to_rows(0, n)
                elif kind == "m":
                    max_tile(0, 0, n)
                elif (kind, n) == ("r", 0):
                    max_rows(0, 0)

            zeros_ok.wait(pe, 2)

            def step(u, par, s, nxt, nxt2, prev):
                v, vpar = u + 1, 1 - par
                tiles = list(range(PIECE[s], PIECE[s + 1])) if nxt else []
                if nxt and s < FILLS:
                    to_rows(v, 2 * s)
                    to_rows(v, 2 * s + 1)
                if s == 1 and prev:
                    weigh(u - 1, vpar, NS - 1)
                scores(u, par, s, 0)
                for k in tiles[:1]:
                    max_tile(v, vpar, k)
                scores(u, par, s, 1)
                for k in tiles[1:2]:
                    max_tile(v, vpar, k)
                if s == 1:
                    max_rows(u, 1)
                for k in tiles[2:3]:
                    max_tile(v, vpar, k)
                if s >= LAG:
                    weigh(u, par, s - LAG)
                elif s == 0 and prev:
                    weigh(u - 1, vpar, NS - 2)
                for k in tiles[3:]:
                    max_tile(v, vpar, k)
                if nxt and s == 5:
                    max_rows(v, 0)
                if s == 7:
                    to_tokens(u, 0)
                if s == 1 and prev:
                    to_tokens(u - 1, 1)
                elif s == 1:
                    claim(turns["o", 1], (o_ok, QC * u, 0))

            def window(u, par, it, nxt):
                if not nxt:
                    return
                for s, kind, n in order:
                    if s < HEAD:
                        free[turns[kind, n]] = [{
                            "t": (t_act if by_act(n) else t_dve, FILLS * (u + 1), n // 2 + 1),
                            "m": (tile_read, NT * (u + 1), n + 1),
                            "r": (mt_read, QC * u, 2),
                            "o": (o_ok, QC * u, 0)}[kind]]

            def end():
                for s in range(NS - LAG, NS):
                    weigh(NU - 1, 1, s)
                to_tokens(NU - 1, 1)
            units(pe, step, window, end)

        @block.scalar
        def _(act):
            exp_ok.give(act)
            o_read.give(act)
            t_act.give(act)

            def take_max(v, c):
                mt_ok.wait(act, QC * v + c + 1)
                row_in[c].wait(act, 16 * HG * v)
                mt_read.by(act.mul(shift[c][:, :], ps[0:TPC * HG, turns["r", c], 0:P], -1.0))

            def exponentials(u, par, s, p):
                c, j = STEPS[s]
                w = CH - first(c, j)
                st_ok.wait(act, NPAIR * (NS * u + s) + p + 1)
                pv_ok.wait(act, NS * u + s - RING + 1)
                bank = S_BANK + 2 * p
                exp_ok.by(act.activation(probs[:, (NS * par + s) % RING, p, :, 0:w], ps[:, bank:bank + 2, 0:w],
                                         ACT.Exp, scale=SCALE))

            def take_o(u, c):
                pv_ok.wait(act, NS * u + (TPC if c == 0 else NS))
                o_read.by(act.copy(o_raw[c][:, :], ps[:, PV_BANK, :]))

            for f in range(FILLS):
                for n in takes(True, f):
                    take(act, act.copy, 0, 0, n)
            shared.wo_in.wait(act, 16)
            shared.wo_ok.by(act.copy(shared.wo_hi[:, :, :], shared.wo[:, :, :]))
            take_max(0, 0)

            def step(u, par, s, nxt, nxt2, prev):
                v, vpar = u + 1, 1 - par
                if nxt and s < FILLS:
                    for n in takes(True, s):
                        take(act, act.copy, v, vpar, n)
                exponentials(u, par, s, 0)
                if s == 1 and prev:
                    take_o(u - 1, 1)
                exponentials(u, par, s, 1)
                if s == 1:
                    take_max(u, 1)
                if nxt and s == 5:
                    take_max(v, 0)
                if s == 5:
                    take_o(u, 0)
            units(act, step, end=lambda: take_o(NU - 1, 1))

        @block.vector
        def _(dve):
            for s in (tile_read, pv_ok, t_dve, o_ok):
                s.give(dve)
            def read_tile(v, k):
                i, part, w, heads = TILES[k]
                tile_ok.wait(dve, NT * v + k + 1)
                n = len(heads)
                tile_read.by(dve.tensor_reduce(maxes[:, part, i, heads[0]:heads[-1] + 1],
                                               ps[:, turns["m", k], 0:n * w].rearrange("p (h k) -> p h k", h=n),
                                               axis=AX.X, op=ALU.max))

            def both_parts(v):
                tile_read.wait(dve, NT * (v + 1))
                maxb_ok.by(dve.tensor_tensor(maxes_b[:, :, :], maxes[:, 0, TPC:, :], maxes[:, 1, TPC:, :], op=ALU.max))

            def normalise(u, c):
                ot_ok.wait(dve, QC * u + c + 1)
                rows = ps[:, turns["o", c], :].rearrange("p (t h d) -> p t h d", t=TPC, d=2 * DH)
                inv = o_inv[:, c]
                inv_ok.by(dve.reciprocal(inv, rows[:, :, :, DH]))
                inv_ok.wait(dve, QC * u + c + 1)
                o_out[c].wait(dve, 16 * u)
                o_ok.by(dve.tensor_tensor(o_nat[c][:, :, :].rearrange("p t (h d) -> p t h d", d=DH), rows[:, :, :, 0:DH],
                                          inv.rearrange("p t (h one) -> p t h one", one=1)
                                          .to_broadcast([P, TPC, HG, DH]), op=ALU.mult))

            for _, kind, n in order:
                if kind == "m":
                    read_tile(0, n)
                elif kind == "t" and not by_act(n):
                    take(dve, dve.tensor_copy, 0, 0, n)
            both_parts(0)
            first_unit.split_lo(dve, 1)
            shared.wo_ok.wait(dve, 1)
            shared.wo_ok.by(dve.tensor_tensor(shared.wo_lo[:, :, :], shared.wo[:, :, :],
                                              shared.wo_hi[:, :, :].bitcast(F32), op=ALU.subtract))

            def step(u, par, s, nxt, nxt2, prev):
                v = u + 1
                if nxt and s < FILLS:
                    for n in takes(False, s):
                        take(dve, dve.tensor_copy, v, 1 - par, n)
                if s == 8:
                    normalise(u, 0)
                if nxt:
                    for k in range(PIECE[s], PIECE[s + 1]):
                        read_tile(v, k)
                    if s == NS - 1:
                        both_parts(v)
                if s == 1 and prev:
                    normalise(u - 1, 1)
                if nxt2 and s == 9:
                    first_unit.split_lo(dve, v + 1)
            units(dve, step, end=lambda: normalise(NU - 1, 1))


def output_block(nc, ps, io, ident, shared):
    out_d = io["out"].rearrange("(o p) (c n) -> c p o n", p=P, n=CH)
    RING, QC = shared.RING, T // CH
    ctx = ExitStack()
    with ctx:
        sb = lambda name, shape, dt=F32: ctx.enter_context(nc.sbuf_tensor(name, shape, dt))
        sem = lambda name, ahead=0: Sem(ctx.enter_context(nc.semaphore(name)), ahead)
        o_hi = [sb(f"o_hi{i}", [P, DC, CH], F32R) for i in range(2)]
        o_lo = [sb(f"o_lo{i}", [P, DC, CH], F32R) for i in range(2)]
        prod = [sb(f"prod_sb{i}", [P, DC, CH]) for i in range(2)]
        res = [sb(f"res{i}", [P, DC, CH]) for i in range(2)]

        passed = sem("o_passed")
        t_ok, hi_ok, lo_ok = sem("o_t_ok"), sem("o_hi_ok", 2), sem("o_lo_ok", 2)
        s_ok = sem("s_ok", 2)
        gated = sem("gated", 2)
        res_ok = sem("res_ok", 2)
        res_out = [sem(f"res_out{i}", 16) for i in range(2)]
        block = ctx.enter_context(nc.Block())

        def chunks(eng, body):
            last = NCHUNK // RING - 1
            with eng.Fori(0, last) as it:
                for r in range(RING):
                    body(it * RING + r, r % 2, r, it, True, True)
            for r in range(RING):
                body(last * RING + r, r % 2, r, last, r < RING - 1, False)

        @block.sync
        def _(eng):
            for s in res_out:
                s.give(eng)

            def body(c, par, r, it, nxt, more):
                res_ok.wait_apart(eng, c + 1, passed)
                res_out[par].by(eng.dma_start(out_d[c], res[par][:, :, :]), 16)
            chunks(eng, body)
            for par in range(2):
                res_out[par].wait(eng, 16 * NCHUNK // 2)

        @block.gpsimd
        def _(eng):
            res_ok.give(eng)
            def body(c, par, r, it, nxt, more):
                gated.wait(eng, c + 1)
                res_out[par].wait_apart(eng, 16 * (it * (RING // 2) + r // 2), passed)
                res_ok.by(eng.tensor_tensor(res[par][:, :, :], prod[par][:, :, :], shared.xt[:, c], op=ALU.add))
            chunks(eng, body)

        @block.tensor
        def _(pe):
            def transposes(c, par, r, it):
                hi_ok.wait(pe, c - 1)
                lo_ok.wait(pe, c - 1)
                shared.heads_in[r].wait(pe, 16 * (it + 1))
                for d in range(DC):
                    for t in range(TPC):
                        last = pe.transpose(ps[:, 2 * par + d, t * P:(t + 1) * P],
                                            shared.heads[:, r, t, d * P:(d + 1) * P], ident[:, :])
                t_ok.by(last)

            def body(c, par, r, it, nxt, more):
                if nxt:
                    transposes(c + 1, 1 - par, (r + 1) % RING, it + (r + 1) // RING)
                hi_ok.wait(pe, c + 1)
                lo_ok.wait(pe, c + 1)
                gated.wait(pe, c - 1)
                for o in range(DC):
                    cols = slice(o * P, (o + 1) * P)
                    terms = [(w[:, d, cols], a[:, d, :]) for d in range(DC)
                             for w, a in ((shared.wo_hi, o_hi[par]), (shared.wo_lo, o_hi[par]),
                                          (shared.wo_hi, o_lo[par]))]
                    for n, (w, a) in enumerate(terms):
                        last = pe.matmul(ps[:, 4 + 2 * par + o, :], w, a, start=(n == 0), stop=(n == len(terms) - 1))
                s_ok.by(last)

            transposes(0, 0, 0, 0)
            chunks(pe, body)

        @block.scalar
        def _(act):
            hi_ok.give(act)

            def high(c, par):
                t_ok.wait(act, c + 1)
                s_ok.wait(act, c - 1)
                hi_ok.by(act.copy(o_hi[par][:, :, :], ps[:, 2 * par:2 * par + 2, :]))
            def body(c, par, r, it, nxt, more):
                if more:
                    b = (it + 1) * (RING // QC) + r // QC
                    shared.o_out[r % QC].wait_apart(act, 16 * NG * (b + 1), passed)
                    shared.load_heads(act, (it + 1) * RING + r, r)
                if nxt:
                    high(c + 1, 1 - par)
            high(0, 0)
            chunks(act, body)

        @block.vector
        def _(dve):
            for s in (lo_ok, gated, s_ok):
                s.give(dve)

            def low(c, par):
                hi_ok.wait(dve, c + 1)
                lo_ok.by(dve.tensor_tensor(o_lo[par][:, :, :], ps[:, 2 * par:2 * par + 2, :],
                                           o_hi[par][:, :, :].bitcast(F32), op=ALU.subtract))

            def body(c, par, r, it, nxt, more):
                if nxt:
                    low(c + 1, 1 - par)
                s_ok.wait(dve, c + 1)
                res_ok.wait_apart(dve, c - 1, passed)
                gated.by(dve.tensor_tensor(prod[par][:, :, :], ps[:, 4 + 2 * par:6 + 2 * par, :], shared.gate[:, c],
                                           op=ALU.mult))
            low(0, 0)
            shared.more_in.wait(dve, 32 * NCHUNK)
            chunks(dve, body)


def build(nc, io):
    scr = {
        "qkv": nc.dram_tensor("scr_qkv", (B, NG, P, TB, 3 * HG * DH), F32).ap(),
        "gate": nc.dram_tensor("scr_gate", (NCHUNK, DC, P, CH), F32).ap(),
        "heads": nc.dram_tensor("scr_heads", (NCHUNK, P, TPC, NG, HG * DH), F32).ap(),
    }
    with nc.psum_tensor("ps", [P, 8, CH], F32) as ps:
        with ExitStack() as ctx:
            first_unit = SlotOperands(nc, ctx, scr)
            ffn_block(nc, ps, io, scr, first_unit)
            shared = OutputOperands(nc, ctx, io, scr)
            attention_block(nc, ps, scr, first_unit, shared)
            output_block(nc, ps, io, first_unit.ident, shared)


def kernel(L0_attn_X, L0_attn_Wq, L0_attn_Wk, L0_attn_Wv, L0_attn_Wo, L0_ffn_SU_ug, L0_ffn_SU_dp,
           L0_ffn_Wscale_ug, L0_ffn_Wscale_dp, L0_ffn_W_up, L0_ffn_W_gate, L0_ffn_W_down):
    import numpy as np
    import concourse.bacc as bacc
    from concourse.bass_utils import run_bass_kernel_spmd

    lay = lambda a: np.ascontiguousarray(np.asarray(a))
    columns = lambda v: lay(np.asarray(v).reshape(-1, P).T)
    x = lay(L0_attn_X).reshape(NTOK, D)

    had = np.ones((1, 1), np.float32)
    while had.shape[0] < P:
        had = np.block([[had, had], [had, -had]])
    theta = np.float32(10000.0) ** (np.float32(-2.0) * np.arange(DH // 2, dtype=np.float32) / np.float32(DH))
    angles = np.arange(T, dtype=np.float32)[:, None] * theta[None, :].astype(np.float32)
    cos = np.repeat(np.cos(angles), 2, axis=1).astype(np.float32)
    sin = np.stack([-np.sin(angles), np.sin(angles)], axis=-1).reshape(T, DH).astype(np.float32)
    tokens = lambda a: lay(a.reshape(TB, P, DH).transpose(1, 0, 2))

    arrays = {
        "x": x,
        "xt": lay(x.T),
        "wqkv": lay(np.concatenate([np.asarray(w).T for w in (L0_attn_Wq, L0_attn_Wk, L0_attn_Wv)], axis=1)),
        "wo": lay(np.asarray(L0_attn_Wo).T),
        "wug": lay(np.concatenate([np.asarray(w).T for w in (L0_ffn_W_up, L0_ffn_W_gate)], axis=1)),
        "wd": lay(np.asarray(L0_ffn_W_down).T),
        "scales": lay(np.concatenate([columns(v) for v in (L0_ffn_SU_ug, L0_ffn_SU_dp, L0_ffn_Wscale_ug,
                                                           L0_ffn_Wscale_dp)], axis=1)),
        "had": lay(had.astype(np.float32)),
        "cos_sin": lay(np.stack([tokens(cos), tokens(sin)], axis=1)),
    }
    nc = bacc.Bacc("TRN2", target_bir_lowering=False, num_devices=1)
    io = {n: nc.dram_tensor("in_" + n, a.shape, mybir.dt.from_np(a.dtype), kind="ExternalInput").ap()
          for n, a in arrays.items()}
    io["out"] = nc.dram_tensor("out_t", (D, NTOK), F32, kind="ExternalOutput").ap()
    build(nc, io)
    r = run_bass_kernel_spmd(nc, [{"in_" + n: a for n, a in arrays.items()}], core_ids=[0])
    return np.ascontiguousarray(r.results[0]["out_t"].T).reshape(B, T, D)
```
